# Optimizing a Trainium2 kernel written in Bass

```python
import numpy as np
import jax
import jax.numpy as jnp

def _softmax(x, axis=-1):
    return jax.nn.softmax(x, axis=axis)

def _gelu(x):
    return jax.nn.gelu(x, approximate=True)

def _silu(x):
    return jax.nn.silu(x)

def _sigmoid(x):
    return jax.nn.sigmoid(x)

def _layernorm(x, axis=-1, eps=1e-05):
    m = jnp.mean(x, axis=axis, keepdims=True)
    v = jnp.var(x, axis=axis, keepdims=True)
    return (x - m) / jnp.sqrt(v + eps)

def _scatter_add(tgt, idx, src, axis=0):
    return tgt.at[idx].add(src)

def _segment_sum(src, seg, n):
    return jax.ops.segment_sum(src, seg, n)
kernel_name = 'mk_dlrm_tower_d1_rec_r8_34e5f5'

def setup_inputs(seed: int=0):
    np.random.seed(seed)
    _w = jnp.asarray

    def _rec_inputs():
        import jax
        import jax.numpy as jnp
        _tk = jax.random.key(seed)
        dense_ctx = jax.random.normal(jax.random.fold_in(_tk, 190), (1024, 16), jnp.float32)
        ids = jnp.stack([jax.random.randint(jax.random.fold_in(_tk, 200 + f), (1024,), 0, v, jnp.int32) for f, v in enumerate([12500, 125000, 1250, 125000, 12500, 125000, 125000, 1000, 1250, 12500, 12500, 1000, 1000, 125000, 125000, 125000, 1000, 125000, 1250, 1000, 125000, 1000, 1250, 12500, 125000, 125000, 1250, 1000, 1250, 12500, 125000, 1250, 125000, 1000, 125000, 1000, 1000, 12500, 12500])], axis=1)
        tbl_0 = 0.05 * jax.random.normal(jax.random.fold_in(_tk, 500 + 0), (12500, 16), jnp.float32)
        tbl_1 = 0.05 * jax.random.normal(jax.random.fold_in(_tk, 500 + 1), (125000, 16), jnp.float32)
        tbl_2 = 0.05 * jax.random.normal(jax.random.fold_in(_tk, 500 + 2), (1250, 16), jnp.float32)
        tbl_3 = 0.05 * jax.random.normal(jax.random.fold_in(_tk, 500 + 3), (125000, 16), jnp.float32)
        tbl_4 = 0.05 * jax.random.normal(jax.random.fold_in(_tk, 500 + 4), (12500, 16), jnp.float32)
        tbl_5 = 0.05 * jax.random.normal(jax.random.fold_in(_tk, 500 + 5), (125000, 16), jnp.float32)
        tbl_6 = 0.05 * jax.random.normal(jax.random.fold_in(_tk, 500 + 6), (125000, 16), jnp.float32)
        tbl_7 = 0.05 * jax.random.normal(jax.random.fold_in(_tk, 500 + 7), (1000, 16), jnp.float32)
        tbl_8 = 0.05 * jax.random.normal(jax.random.fold_in(_tk, 500 + 8), (1250, 16), jnp.float32)
        tbl_9 = 0.05 * jax.random.normal(jax.random.fold_in(_tk, 500 + 9), (12500, 16), jnp.float32)
        tbl_10 = 0.05 * jax.random.normal(jax.random.fold_in(_tk, 500 + 10), (12500, 16), jnp.float32)
        tbl_11 = 0.05 * jax.random.normal(jax.random.fold_in(_tk, 500 + 11), (1000, 16), jnp.float32)
        tbl_12 = 0.05 * jax.random.normal(jax.random.fold_in(_tk, 500 + 12), (1000, 16), jnp.float32)
        tbl_13 = 0.05 * jax.random.normal(jax.random.fold_in(_tk, 500 + 13), (125000, 16), jnp.float32)
        tbl_14 = 0.05 * jax.random.normal(jax.random.fold_in(_tk, 500 + 14), (125000, 16), jnp.float32)
        tbl_15 = 0.05 * jax.random.normal(jax.random.fold_in(_tk, 500 + 15), (125000, 16), jnp.float32)
        tbl_16 = 0.05 * jax.random.normal(jax.random.fold_in(_tk, 500 + 16), (1000, 16), jnp.float32)
        tbl_17 = 0.05 * jax.random.normal(jax.random.fold_in(_tk, 500 + 17), (125000, 16), jnp.float32)
        tbl_18 = 0.05 * jax.random.normal(jax.random.fold_in(_tk, 500 + 18), (1250, 16), jnp.float32)
        tbl_19 = 0.05 * jax.random.normal(jax.random.fold_in(_tk, 500 + 19), (1000, 16), jnp.float32)
        tbl_20 = 0.05 * jax.random.normal(jax.random.fold_in(_tk, 500 + 20), (125000, 16), jnp.float32)
        tbl_21 = 0.05 * jax.random.normal(jax.random.fold_in(_tk, 500 + 21), (1000, 16), jnp.float32)
        tbl_22 = 0.05 * jax.random.normal(jax.random.fold_in(_tk, 500 + 22), (1250, 16), jnp.float32)
        tbl_23 = 0.05 * jax.random.normal(jax.random.fold_in(_tk, 500 + 23), (12500, 16), jnp.float32)
        tbl_24 = 0.05 * jax.random.normal(jax.random.fold_in(_tk, 500 + 24), (125000, 16), jnp.float32)
        tbl_25 = 0.05 * jax.random.normal(jax.random.fold_in(_tk, 500 + 25), (125000, 16), jnp.float32)
        tbl_26 = 0.05 * jax.random.normal(jax.random.fold_in(_tk, 500 + 26), (1250, 16), jnp.float32)
        tbl_27 = 0.05 * jax.random.normal(jax.random.fold_in(_tk, 500 + 27), (1000, 16), jnp.float32)
        tbl_28 = 0.05 * jax.random.normal(jax.random.fold_in(_tk, 500 + 28), (1250, 16), jnp.float32)
        tbl_29 = 0.05 * jax.random.normal(jax.random.fold_in(_tk, 500 + 29), (12500, 16), jnp.float32)
        tbl_30 = 0.05 * jax.random.normal(jax.random.fold_in(_tk, 500 + 30), (125000, 16), jnp.float32)
        tbl_31 = 0.05 * jax.random.normal(jax.random.fold_in(_tk, 500 + 31), (1250, 16), jnp.float32)
        tbl_32 = 0.05 * jax.random.normal(jax.random.fold_in(_tk, 500 + 32), (125000, 16), jnp.float32)
        tbl_33 = 0.05 * jax.random.normal(jax.random.fold_in(_tk, 500 + 33), (1000, 16), jnp.float32)
        tbl_34 = 0.05 * jax.random.normal(jax.random.fold_in(_tk, 500 + 34), (125000, 16), jnp.float32)
        tbl_35 = 0.05 * jax.random.normal(jax.random.fold_in(_tk, 500 + 35), (1000, 16), jnp.float32)
        tbl_36 = 0.05 * jax.random.normal(jax.random.fold_in(_tk, 500 + 36), (1000, 16), jnp.float32)
        tbl_37 = 0.05 * jax.random.normal(jax.random.fold_in(_tk, 500 + 37), (12500, 16), jnp.float32)
        tbl_38 = 0.05 * jax.random.normal(jax.random.fold_in(_tk, 500 + 38), (12500, 16), jnp.float32)
        _rk = jax.random.fold_in(_tk, 7)
        W_top1 = 0.0606339 * jax.random.normal(jax.random.fold_in(_tk, 801), (272, 512), jnp.float32)
        W_top2 = 0.0441942 * jax.random.normal(jax.random.fold_in(_tk, 802), (512, 256), jnp.float32)
        W_top3 = 0.0625 * jax.random.normal(jax.random.fold_in(_tk, 803), (256, 1), jnp.float32)
        b_top1 = jnp.zeros((512,), jnp.float32)
        b_top2 = jnp.zeros((256,), jnp.float32)
        return (dense_ctx, ids, tbl_0, tbl_1, tbl_2, tbl_3, tbl_4, tbl_5, tbl_6, tbl_7, tbl_8, tbl_9, tbl_10, tbl_11, tbl_12, tbl_13, tbl_14, tbl_15, tbl_16, tbl_17, tbl_18, tbl_19, tbl_20, tbl_21, tbl_22, tbl_23, tbl_24, tbl_25, tbl_26, tbl_27, tbl_28, tbl_29, tbl_30, tbl_31, tbl_32, tbl_33, tbl_34, tbl_35, tbl_36, tbl_37, tbl_38, W_top1, b_top1, W_top2, b_top2, W_top3)
    dense_ctx, ids, tbl_0, tbl_1, tbl_2, tbl_3, tbl_4, tbl_5, tbl_6, tbl_7, tbl_8, tbl_9, tbl_10, tbl_11, tbl_12, tbl_13, tbl_14, tbl_15, tbl_16, tbl_17, tbl_18, tbl_19, tbl_20, tbl_21, tbl_22, tbl_23, tbl_24, tbl_25, tbl_26, tbl_27, tbl_28, tbl_29, tbl_30, tbl_31, tbl_32, tbl_33, tbl_34, tbl_35, tbl_36, tbl_37, tbl_38, W_top1, b_top1, W_top2, b_top2, W_top3 = _rec_inputs()

    def _L0_rec_setup():
        import jax, jax.numpy as jnp
        import numpy as np
        B, M, D = (1024, 39, 16)
        S1, S2 = (128, 128)

        def _cin_layer(x0, xk, W, b):
            out = jnp.einsum('bhd,bmd,shm->bsd', xk, x0, W) + b[None, :, None]
            return jax.nn.relu(out)
        key = jax.random.key(seed)
        k0, k1, k2 = jax.random.split(key, 3)
        x0 = jax.random.normal(k0, (B, M, D), dtype=jnp.float32)
        W1 = jax.random.normal(k1, (S1, M, M), dtype=jnp.float32) * 0.05
        b1 = jnp.zeros((S1,), dtype=jnp.float32)
        W2 = jax.random.normal(k2, (S2, S1, M), dtype=jnp.float32) * 0.05
        b2 = jnp.zeros((S2,), dtype=jnp.float32)
        return {'x0': x0, 'W1': W1, 'b1': b1, 'W2': W2, 'b2': b2}
    _L0_rec_all = _L0_rec_setup()
    _L0_rec_in = {k: v for k, v in _L0_rec_all.items() if k in ('W1', 'b1', 'W2', 'b2')}
    del _L0_rec_all
    return {'dense_ctx': dense_ctx, 'ids': ids, 'tbl_0': tbl_0, 'tbl_1': tbl_1, 'tbl_2': tbl_2, 'tbl_3': tbl_3, 'tbl_4': tbl_4, 'tbl_5': tbl_5, 'tbl_6': tbl_6, 'tbl_7': tbl_7, 'tbl_8': tbl_8, 'tbl_9': tbl_9, 'tbl_10': tbl_10, 'tbl_11': tbl_11, 'tbl_12': tbl_12, 'tbl_13': tbl_13, 'tbl_14': tbl_14, 'tbl_15': tbl_15, 'tbl_16': tbl_16, 'tbl_17': tbl_17, 'tbl_18': tbl_18, 'tbl_19': tbl_19, 'tbl_20': tbl_20, 'tbl_21': tbl_21, 'tbl_22': tbl_22, 'tbl_23': tbl_23, 'tbl_24': tbl_24, 'tbl_25': tbl_25, 'tbl_26': tbl_26, 'tbl_27': tbl_27, 'tbl_28': tbl_28, 'tbl_29': tbl_29, 'tbl_30': tbl_30, 'tbl_31': tbl_31, 'tbl_32': tbl_32, 'tbl_33': tbl_33, 'tbl_34': tbl_34, 'tbl_35': tbl_35, 'tbl_36': tbl_36, 'tbl_37': tbl_37, 'tbl_38': tbl_38, 'W_top1': W_top1, 'b_top1': b_top1, 'W_top2': W_top2, 'b_top2': b_top2, 'W_top3': W_top3, 'L0_rec_W1': _L0_rec_in['W1'], 'L0_rec_b1': _L0_rec_in['b1'], 'L0_rec_W2': _L0_rec_in['W2'], 'L0_rec_b2': _L0_rec_in['b2']}

def reference(dense_ctx, ids, tbl_0, tbl_1, tbl_2, tbl_3, tbl_4, tbl_5, tbl_6, tbl_7, tbl_8, tbl_9, tbl_10, tbl_11, tbl_12, tbl_13, tbl_14, tbl_15, tbl_16, tbl_17, tbl_18, tbl_19, tbl_20, tbl_21, tbl_22, tbl_23, tbl_24, tbl_25, tbl_26, tbl_27, tbl_28, tbl_29, tbl_30, tbl_31, tbl_32, tbl_33, tbl_34, tbl_35, tbl_36, tbl_37, tbl_38, W_top1, b_top1, W_top2, b_top2, W_top3, L0_rec_W1, L0_rec_b1, L0_rec_W2, L0_rec_b2):
    import jax
    import jax.numpy as jnp

    def _L0_rec_ref(x0, W1, b1, W2, b2):
        import jax, jax.numpy as jnp
        import numpy as np
        B, M, D = (1024, 39, 16)
        S1, S2 = (128, 128)

        def _cin_layer(x0, xk, W, b):
            out = jnp.einsum('bhd,bmd,shm->bsd', xk, x0, W) + b[None, :, None]
            return jax.nn.relu(out)
        x1 = _cin_layer(x0, x0, W1, b1)
        x2 = _cin_layer(x0, x1, W2, b2)
        p1 = x1.sum(axis=-1)
        p2 = x2.sum(axis=-1)
        return jnp.concatenate([p1, p2], axis=-1)
    e = jnp.stack([tbl_0[ids[:, 0]], tbl_1[ids[:, 1]], tbl_2[ids[:, 2]], tbl_3[ids[:, 3]], tbl_4[ids[:, 4]], tbl_5[ids[:, 5]], tbl_6[ids[:, 6]], tbl_7[ids[:, 7]], tbl_8[ids[:, 8]], tbl_9[ids[:, 9]], tbl_10[ids[:, 10]], tbl_11[ids[:, 11]], tbl_12[ids[:, 12]], tbl_13[ids[:, 13]], tbl_14[ids[:, 14]], tbl_15[ids[:, 15]], tbl_16[ids[:, 16]], tbl_17[ids[:, 17]], tbl_18[ids[:, 18]], tbl_19[ids[:, 19]], tbl_20[ids[:, 20]], tbl_21[ids[:, 21]], tbl_22[ids[:, 22]], tbl_23[ids[:, 23]], tbl_24[ids[:, 24]], tbl_25[ids[:, 25]], tbl_26[ids[:, 26]], tbl_27[ids[:, 27]], tbl_28[ids[:, 28]], tbl_29[ids[:, 29]], tbl_30[ids[:, 30]], tbl_31[ids[:, 31]], tbl_32[ids[:, 32]], tbl_33[ids[:, 33]], tbl_34[ids[:, 34]], tbl_35[ids[:, 35]], tbl_36[ids[:, 36]], tbl_37[ids[:, 37]], tbl_38[ids[:, 38]]], axis=1)
    z = _L0_rec_ref(e, L0_rec_W1, L0_rec_b1, L0_rec_W2, L0_rec_b2)
    z = z.reshape(z.shape[0], -1)
    h = jnp.concatenate([z, dense_ctx], axis=1)
    h = jnp.maximum(h @ W_top1 + b_top1, 0.0)
    h = jnp.maximum(h @ W_top2 + b_top2, 0.0)
    y = h @ W_top3
    return y

_drawn_inputs = setup_inputs


def setup_inputs(seed=0):
    import zlib

    import numpy as np

    out = dict(_drawn_inputs(seed))
    spreads = {'b_top1': (0.0, 0.1),
     'b_top2': (0.0, 0.1),
     'L0_rec_b1': (0.0, 0.1),
     'L0_rec_b2': (0.0, 0.1)}
    factors = {'tbl_0': 4.728,
     'tbl_1': 4.313,
     'tbl_2': 7.188,
     'tbl_3': 6.273,
     'tbl_4': 6.957,
     'tbl_5': 7.293,
     'tbl_6': 5.734,
     'tbl_7': 4.671,
     'tbl_8': 8.0,
     'tbl_9': 7.611,
     'tbl_10': 6.232,
     'tbl_11': 5.794,
     'tbl_12': 5.226,
     'tbl_14': 8.0,
     'tbl_15': 6.6,
     'tbl_16': 7.627,
     'tbl_17': 4.618,
     'tbl_18': 5.551,
     'tbl_19': 4.531,
     'tbl_20': 8.0,
     'tbl_21': 3.376,
     'tbl_22': 8.0,
     'tbl_23': 7.705,
     'tbl_24': 7.611,
     'tbl_25': 5.066,
     'tbl_26': 4.279,
     'tbl_27': 6.408,
     'tbl_28': 7.938,
     'tbl_29': 5.296,
     'tbl_30': 5.176,
     'tbl_31': 2.954,
     'tbl_32': 8.0,
     'tbl_33': 7.492,
     'tbl_34': 7.092,
     'tbl_35': 7.371,
     'tbl_36': 8.0,
     'tbl_37': 8.0,
     'tbl_38': 6.428,
     'tbl_13': 4.173}
    for name, (base, spread) in spreads.items():
        noise = np.random.default_rng([zlib.crc32(name.encode()), seed]).standard_normal(out[name].shape)
        drawn = base * np.exp(spread * noise) if base else spread * noise
        out[name] = jnp.asarray(drawn.astype(out[name].dtype))
    for name, factor in factors.items():
        out[name] = (out[name] * factor).astype(out[name].dtype)
    return out
```

```python
from contextlib import ExitStack

import concourse.bass as bass
from concourse import mybir

F32 = mybir.dt.float32
F32R = mybir.dt.float32r
U32 = mybir.dt.uint32
ALU = mybir.AluOpType
ACT = mybir.ActivationFunctionType
AX_X = mybir.AxisListType.X

P = 128
D = 16
BANK = 512
MB = BANK // P
RING = 5
ACT_CREDIT = 3
DVE_CREDIT = 2
FOLD_CREDIT = 2
PREP = 4


def build(nc, dense_ctx, ids, tables, W_top1, b_top1, W_top2, b_top2, W_top3, W1, b1, W2, b2, eye, out):
    B, DC = dense_ctx.shape
    S, M, _ = W1.shape
    NB = B // P
    SHIFTS = (M + 1) // 2
    PAIRS = SHIFTS * M
    CH = 7
    CK = (PAIRS + CH - 1) // CH
    EXT = M + SHIFTS - 1
    NG = (M + MB - 1) // MB
    H1, H2 = W_top1.shape[1], W_top2.shape[1]
    act_banks = [q for q in range(NG) if q % RING % 2 == 0]
    dve_banks = [q for q in range(NG) if q % RING % 2 == 1]
    NA, NV = len(act_banks), len(dve_banks)
    assert (S, NG, NA, NV, D) == (P, 2 * RING, 6, 4, 16)

    def fields(q):
        return range(MB * q, min(MB * q + MB, M))

    with ExitStack() as ctx:
        def sb(name, shape, dt=F32):
            return ctx.enter_context(nc.sbuf_tensor(name, shape, dt))

        def sem(name):
            return ctx.enter_context(nc.semaphore(name))

        y_bank = ctx.enter_context(nc.psum_tensor("y_bank", [P, RING, BANK], F32))
        turn_bank = ctx.enter_context(nc.psum_tensor("turn_bank", [P, 2, BANK], F32))
        x1_bank = ctx.enter_context(nc.psum_tensor("x1_bank", [P, BANK], F32))

        ident = sb("ident", [P, P])
        idx = sb("idx", [P, M], U32)
        emb = sb("emb", [P, M * D])
        x0 = sb("x0", [P, D // 4, 4, EXT])
        pairs = sb("pairs", [P, 2, CH * CK])
        pairs_t = sb("pairs_t", [P, 2, CH, 2 * P])
        w1_ext = sb("w1_ext", [P, EXT, EXT])
        w1_fold = sb("w1_fold", [P, CH * CK])
        w1_t = sb("w1_t", [P, CH, S])
        w2_raw = sb("w2_raw", [P, P, M])
        w2_high = sb("w2_high", [P, M * S], F32R)
        w2_low = sb("w2_low", [P, M * S], F32R)
        b1_col = sb("b1_col", [P, 1])
        b2_row = sb("b2_row", [P, S])
        x1_full = sb("x1_full", [P, D, P])
        x1_high = sb("x1_high", [P, 2, 2 * P], F32R)
        x1_low = sb("x1_low", [P, 2, 2 * P], F32R)
        scaled = sb("scaled", [P, 2, NA, BANK])
        pool_sum = sb("pool_sum", [P, 2, BANK])
        mac = sb("mac", [P, 2, 2 * S])
        fold4 = sb("fold4", [P, BANK])
        fold2 = sb("fold2", [P, 2 * S])
        fold1 = sb("fold1", [P, S])
        p2_part = sb("p2_part", [P, S])
        p1_all = sb("p1_all", [P, B])
        p2_all = sb("p2_all", [P, NB * S])
        p2_t = sb("p2_t", [P, B])
        dense = sb("dense", [P, NB, DC])
        dense_t = sb("dense_t", [P, B])
        wt1 = sb("wt1", [P, 3, H1])
        wt2 = sb("wt2", [P, H1 // P, H2])
        wt3 = sb("wt3", [P, H2 // P])
        bt1 = sb("bt1", [P, H1 // P])
        bt2 = sb("bt2", [P, H2 // P])
        h1 = sb("h1", [P, H1 // P, BANK])
        h2 = sb("h2", [P, H2 // P, BANK])
        y_row = sb("y_row", [1, B])

        ids_in = sem("ids_in")
        ident_in = sem("ident_in")
        w1_in = sem("w1_in")
        w2_in = sem("w2_in")
        small_in = sem("small_in")
        gathered = sem("gathered")
        w1_step = sem("w1_step")
        w1_turned = sem("w1_turned")
        w1_copied = sem("w1_copied")
        w2_turned = sem("w2_turned")
        w2_rounded = sem("w2_rounded")
        w2_split = sem("w2_split")
        dense_turned = sem("dense_turned")
        dense_copied = sem("dense_copied")
        staged = sem("staged")
        paired = sem("paired")
        turned = sem("turned")
        evacuated = sem("evacuated")
        l1_done = sem("l1_done")
        x1_rounded = sem("x1_rounded")
        x1_split = sem("x1_split")
        y_for_act = sem("y_for_act")
        y_for_dve = sem("y_for_dve")
        act_scaled = sem("act_scaled")
        mac_done = sem("mac_done")
        dve_read = sem("dve_read")
        pool_added = sem("pool_added")
        fold_step = sem("fold_step")
        folded = sem("folded")
        p1_reduced = sem("p1_reduced")
        p2_turned = sem("p2_turned")
        p2_copied = sem("p2_copied")
        top_sum = sem("top_sum")
        top_act = sem("top_act")
        y_out = sem("y_out")

        block = ctx.enter_context(nc.Block())

        @block.sync
        def _(sp):
            sp.dma_start(idx[:, :], ids[0:P, :]).then_inc(ids_in, 16)
            sp.dma_start(w1_ext[:, 0:M, 0:M], W1).then_inc(w1_in, 16)
            sp.dma_start(ident[:, :], eye).then_inc(ident_in, 16)
            sp.dma_start(w2_raw[:, :, :], W2).then_inc(w2_in, 16)
            small = [
                (b1_col[:, :], b1.rearrange("(s o) -> s o", o=1)),
                (b2_row[:, :], b2.rearrange("(o s) -> o s", o=1).to_broadcast([P, S])),
                (dense[:, :, :], dense_ctx.rearrange("(t p) c -> p t c", p=P)),
                (wt1[:, 0:2, :], W_top1[0:2 * P, :].rearrange("(c p) n -> p c n", p=P)),
                (wt1[0:DC, 2, :], W_top1[2 * P:2 * P + DC, :]),
                (wt2[:, :, :], W_top2.rearrange("(c p) n -> p c n", p=P)),
                (wt3[:, :], W_top3.rearrange("(c p) o -> p (c o)", p=P)),
                (bt1[:, :], b_top1.rearrange("(c p) -> p c", p=P)),
                (bt2[:, :], b_top2.rearrange("(c p) -> p c", p=P)),
            ]
            with nc.allow_non_contiguous_dma(reason="a few hundred bias and W_top3 elements"):
                for dst, src in small:
                    sp.dma_start(dst, src).then_inc(small_in, 16)
            with sp.Fori(0, NB - 1, 1) as i:
                sp.wait_ge(gathered, i * (16 * M) + 16 * M)
                sp.dma_start(idx[:, :], ids[bass.ds(i * P + P, P), :]).then_inc(ids_in, 16)
            sp.wait_ge(top_act, 2 * (H1 // P + H2 // P + 1))
            sp.dma_start(out.rearrange("b o -> o b"), y_row[:, :]).then_inc(y_out, 16)
            sp.wait_ge(y_out, 16)
        SMALL = 16 * 9

        @block.gpsimd
        def _(pool):
            def gather(f):
                pool.indirect_dma_start(emb[:, f * D:(f + 1) * D], None, tables[f],
                                        bass.IndirectOffsetOnAxis(ap=idx[:, f:f + 1], axis=0)).then_inc(gathered, 16)

            def products(i, t):
                i, t = (i + 1, t - D) if t >= D else (i, t)
                g, dd = t // 4, t % 4
                pool.wait_ge(staged, i * 8 + (2 * g + 2))
                if not (isinstance(i, int) and i == 0 and t < 2):
                    pool.wait_ge(turned, i * (2 * D) + (2 * t - 2))
                base = x0[:, g, dd, 0:M]
                near = base.unsqueeze(1).to_broadcast([P, SHIFTS, M])
                far = bass.AP(base.tensor, base.offset, [list(base.ap[0]), [1, SHIFTS], [1, M]])
                dst = pairs[:, t % 2, 0:PAIRS].rearrange("p (k h) -> p k h", h=M)
                pool.tensor_tensor(dst, near, far, ALU.mult).then_inc(paired, 1)

            def add_first(i, t):
                pool.wait_ge(act_scaled, i * (NA * D) + (NA * t + 2 + ACT_CREDIT))
                pool.wait_ge(folded, i * D + (t - 1 + FOLD_CREDIT))
                pool.tensor_tensor(pool_sum[:, t % 2, :], scaled[:, t % 2, 0, :], scaled[:, t % 2, 1, :],
                                   ALU.add).then_inc(pool_added, 1)

            FIRST, LAST = 1, 9
            share = [M * n // (LAST - FIRST + 1) for n in range(LAST - FIRST + 2)]

            def body(i, last=False):
                for t in range(D):
                    if not last and t == FIRST:
                        pool.wait_ge(staged, i * 8 + 8)
                        pool.wait_ge(ids_in, i * 16 + 32)
                    if not (last and t + PREP >= D):
                        products(i, t + PREP)
                    if not last and FIRST <= t <= LAST:
                        for f in range(share[t - FIRST], share[t - FIRST + 1]):
                            gather(f)
                    add_first(i, t)

            pool.wait_ge(ids_in, 16)
            for f in range(M):
                gather(f)
            pool.wait_ge(w1_step, 1)
            for t in range(PREP):
                products(0, t)
            with pool.Fori(0, NB - 1, 1) as i:
                body(i)
            body(NB - 1, last=True)

        @block.tensor
        def _(pe):
            def turn(i, t, half):
                i, t = (i + 1, t - D) if t >= D else (i, t)
                if half == 0:
                    pe.wait_ge(paired, i * D + (t + 1))
                if not (isinstance(i, int) and i == 0 and t == 0):
                    pe.wait_ge(evacuated, i * (2 * D) + (2 * t - 1 + half))
                chunks = range(0, 4) if half == 0 else range(4, CH)
                for n, c in enumerate(chunks):
                    mm = pe.transpose(turn_bank[0:CK, half, n * P:(n + 1) * P],
                                      pairs[:, t % 2, c * CK:(c + 1) * CK], ident[:, :])
                mm.then_inc(turned, 1)

            def layer1(i, pair, c):
                i, pair = (i + 1, pair - D // 2) if pair >= D // 2 else (i, pair)
                if c == 0:
                    pe.wait_ge(evacuated, i * (2 * D) + (4 * pair + 4))
                    if not (isinstance(i, int) and i == 0 and pair == 0):
                        pe.wait_ge(x1_rounded, i * (D // 2) + pair)
                mm = pe.matmul(x1_bank[:, 0:2 * P], w1_t[0:CK, c, :], pairs_t[0:CK, pair % 2, c, :],
                               start=(c == 0), stop=(c == CH - 1))
                if c == CH - 1:
                    mm.then_inc(l1_done, 1)

            def layer2(i, t, q):
                bank, n = q % RING, S * len(fields(q))
                if q == 0 and t % 2 == 0:
                    pe.wait_ge(x1_split, i * (D // 2) + (t // 2 + 1))
                if q in act_banks:
                    pe.wait_ge(act_scaled, i * (NA * D) + (NA * t + act_banks.index(q) + 1))
                else:
                    pe.wait_ge(dve_read, i * (NV * D) + (NV * t + dve_banks.index(q) + 1))
                cols = slice(MB * S * q, MB * S * q + n)
                high = x1_high[:, t // 2 % 2, t % 2 * P:(t % 2 + 1) * P]
                low = x1_low[:, t // 2 % 2, t % 2 * P:(t % 2 + 1) * P]
                dst = y_bank[:, bank, 0:n]
                pe.matmul(dst, low, w2_high[:, cols], start=True, stop=False)
                pe.matmul(dst, high, w2_low[:, cols], start=False, stop=False)
                mm = pe.matmul(dst, high, w2_high[:, cols], start=False, stop=True)
                mm.then_inc(y_for_act if q in act_banks else y_for_dve, 1)

            BEHIND = [
                {0: ("l1", 0), 1: ("turn", 0), 2: ("l1", 1), 4: ("l1", 2), 5: ("turn", 1), 7: ("l1", 3)},
                {0: ("l1", 4), 1: ("l1", 5), 2: ("l1", 6), 5: ("turn", 0), 7: ("turn", 1)},
            ]

            def body(i, last=False):
                for t in range(D):
                    for q in range(NG):
                        layer2(i, t, q)
                        what, n = BEHIND[t % 2].get(q, (None, 0))
                        if what == "l1" and not (last and t // 2 + 1 >= D // 2):
                            layer1(i, t // 2 + 1, n)
                        if what == "turn" and not (last and t + PREP >= D):
                            turn(i, t + PREP, n)

            pe.wait_ge(ident_in, 16)
            pe.wait_ge(w2_in, 16)
            for q in range(NG):
                if q >= RING:
                    pe.wait_ge(w2_split, q - RING + 1)
                for n, m in enumerate(fields(q)):
                    mm = pe.transpose(y_bank[:, q % RING, n * P:(n + 1) * P], w2_raw[:, :, m], ident[:, :])
                mm.then_inc(w2_turned, 1)
            pe.wait_ge(w1_step, 6)
            for c in range(CH):
                mm = pe.transpose(turn_bank[0:CK, c // 4, c % 4 * P:(c % 4 + 1) * P],
                                  w1_fold[:, c * CK:(c + 1) * CK], ident[:, :])
            mm.then_inc(w1_turned, 1)
            pe.wait_ge(small_in, SMALL)
            for half in range(2):
                if half:
                    pe.wait_ge(dense_copied, 1)
                for n in range(NB // 2):
                    mm = pe.transpose(x1_bank[0:DC, n * P:(n + 1) * P], dense[:, half * NB // 2 + n, :], ident[:, :])
                mm.then_inc(dense_turned, 1)
            pe.wait_ge(w1_copied, 1)
            for t in range(PREP):
                turn(0, t, 0)
                turn(0, t, 1)
            pe.wait_ge(dense_copied, 2)
            for c in range(CH):
                layer1(0, 0, c)
            pe.wait_ge(w2_split, NG)
            with pe.Fori(0, NB - 1, 1) as i:
                body(i)
            body(NB - 1, last=True)

            pe.wait_ge(folded, NB * D + FOLD_CREDIT)
            for half in range(2):
                for n in range(NB // 2):
                    b = half * NB // 2 + n
                    mm = pe.transpose(turn_bank[:, half, n * P:(n + 1) * P], p2_all[:, b * S:(b + 1) * S], ident[:, :])
                mm.then_inc(p2_turned, 1)
            pe.wait_ge(p1_reduced, NB)
            pe.wait_ge(act_scaled, NB * NA * D + ACT_CREDIT)
            step = 0
            for half in range(2):
                rows = slice(half * BANK, (half + 1) * BANK)
                pe.wait_ge(p2_copied, half + 1)
                for c in range(H1 // P):
                    if step >= RING:
                        pe.wait_ge(top_act, step - RING + 1)
                    dst = y_bank[:, step % RING, :]
                    cols = slice(c * P, (c + 1) * P)
                    pe.matmul(dst, wt1[:, 0, cols], p1_all[:, rows], start=True, stop=False)
                    pe.matmul(dst, wt1[0:DC, 2, cols], dense_t[0:DC, rows], start=False, stop=False)
                    pe.matmul(dst, wt1[:, 1, cols], p2_t[:, rows], start=False, stop=True).then_inc(top_sum, 1)
                    step += 1
                pe.wait_ge(top_act, step)
                for c in range(H2 // P):
                    for k in range(H1 // P):
                        mm = pe.matmul(y_bank[:, step % RING, :], wt2[:, k, c * P:(c + 1) * P], h1[:, k, :],
                                       start=(k == 0), stop=(k == H1 // P - 1))
                    mm.then_inc(top_sum, 1)
                    step += 1
                pe.wait_ge(top_act, step)
                for k in range(H2 // P):
                    mm = pe.matmul(y_bank[0:1, step % RING, :], wt3[:, k:k + 1], h2[:, k, :],
                                   start=(k == 0), stop=(k == H2 // P - 1))
                mm.then_inc(top_sum, 1)
                step += 1

        @block.scalar
        def _(act):
            def scale(i, t, a):
                q = act_banks[a]
                if a == 0:
                    act.wait_ge(folded, i * D + (t - 1 + FOLD_CREDIT))
                act.wait_ge(y_for_act, i * (NA * D) + (NA * t + a + 1))
                for n, m in enumerate(fields(q)):
                    ins = act.activation(scaled[:, t % 2, a, n * S:(n + 1) * S], y_bank[:, q % RING, n * S:(n + 1) * S],
                                         ACT.Copy, scale=x0[:, t // 4, t % 4, m:m + 1])
                ins.then_inc(act_scaled, 1)

            def evacuate(i, t, half):
                i, t = (i + 1, t - D) if t >= D else (i, t)
                act.wait_ge(turned, i * (2 * D) + (2 * t + half + 1))
                if t % 2 == 0 and half == 0 and not (isinstance(i, int) and i == 0 and t < 4):
                    act.wait_ge(l1_done, i * (D // 2) + (t // 2 - 1))
                c0, c1 = (0, 4) if half == 0 else (4, CH)
                act.activation(pairs_t[0:CK, t // 2 % 2, c0:c1, t % 2 * P:(t % 2 + 1) * P],
                               turn_bank[0:CK, half, 0:(c1 - c0) * P].rearrange("p (c n) -> p c n", n=P),
                               ACT.Copy).then_inc(evacuated, 1)

            def first_maps(i, pair):
                i, pair = (i + 1, pair - D // 2) if pair >= D // 2 else (i, pair)
                act.wait_ge(l1_done, i * (D // 2) + (pair + 1))
                if pair == 0 and not (isinstance(i, int) and i == 0):
                    act.wait_ge(p1_reduced, i)
                act.activation(x1_full[:, 2 * pair:2 * pair + 2, :],
                               x1_bank[:, 0:2 * P].rearrange("p (d n) -> p d n", n=P),
                               ACT.Relu, bias=b1_col[:, 0:1])
                act.activation(x1_high[:, pair % 2, :], x1_bank[:, 0:2 * P],
                               ACT.Relu, bias=b1_col[:, 0:1]).then_inc(x1_rounded, 1)

            BEHIND = [
                {1: ("evacuate", 0), 3: ("evacuate", 1)},
                {1: ("maps", 0), 3: ("evacuate", 0), 4: ("evacuate", 1)},
            ]

            def body(i, last=False):
                for t in range(D):
                    for a in range(NA):
                        scale(i, t, a)
                        what, n = BEHIND[t % 2].get(a, (None, 0))
                        if what == "maps" and not (last and t // 2 + 1 >= D // 2):
                            first_maps(i, t // 2 + 1)
                        if what == "evacuate" and not (last and t + PREP >= D):
                            evacuate(i, t + PREP, n)

            act.sem_inc(act_scaled, ACT_CREDIT)
            for q in range(NG):
                act.wait_ge(w2_turned, q + 1)
                n = S * len(fields(q))
                act.activation(w2_high[:, MB * S * q:MB * S * q + n], y_bank[:, q % RING, 0:n],
                               ACT.Copy).then_inc(w2_rounded, 1)
            act.wait_ge(w1_turned, 1)
            act.activation(w1_t[0:CK, 0:4, :], turn_bank[0:CK, 0, :].rearrange("p (c n) -> p c n", n=P), ACT.Copy)
            act.activation(w1_t[0:CK, 4:CH, :], turn_bank[0:CK, 1, 0:(CH - 4) * P].rearrange("p (c n) -> p c n", n=P),
                           ACT.Copy).then_inc(w1_copied, 1)
            act.wait_ge(small_in, SMALL)
            for half in range(2):
                act.wait_ge(dense_turned, half + 1)
                act.activation(dense_t[0:DC, half * BANK:(half + 1) * BANK], x1_bank[0:DC, :],
                               ACT.Copy).then_inc(dense_copied, 1)
            for t in range(PREP):
                evacuate(0, t, 0)
                evacuate(0, t, 1)
            first_maps(0, 0)
            with act.Fori(0, NB - 1, 1) as i:
                body(i)
            body(NB - 1, last=True)

            for half in range(2):
                act.wait_ge(p2_turned, half + 1)
                act.activation(p2_t[:, half * BANK:(half + 1) * BANK], turn_bank[:, half, :],
                               ACT.Copy).then_inc(p2_copied, 1)
            step = 0
            for half in range(2):
                for c in range(H1 // P):
                    act.wait_ge(top_sum, step + 1)
                    act.activation(h1[:, c, :], y_bank[:, step % RING, :], ACT.Relu,
                                   bias=bt1[:, c:c + 1]).then_inc(top_act, 1)
                    step += 1
                for c in range(H2 // P):
                    act.wait_ge(top_sum, step + 1)
                    act.activation(h2[:, c, :], y_bank[:, step % RING, :], ACT.Relu,
                                   bias=bt2[:, c:c + 1]).then_inc(top_act, 1)
                    step += 1
                act.wait_ge(top_sum, step + 1)
                act.activation(y_row[:, half * BANK:(half + 1) * BANK], y_bank[0:1, step % RING, :],
                               ACT.Copy).then_inc(top_act, 1)
                step += 1

        @block.vector
        def _(dve):
            def macs(i, t, v, part):
                i, t = (i + 1, t - D) if t >= D else (i, t)
                q = dve_banks[v]
                if part == 0:
                    dve.wait_ge(y_for_dve, i * (NV * D) + (NV * t + v + 1))
                for n in (2 * part, 2 * part + 1):
                    m = MB * q + n
                    src = y_bank[:, q % RING, n * S:(n + 1) * S]
                    dst = mac[:, t % 2, n % 2 * S:(n % 2 + 1) * S]
                    x = x0[:, t // 4, t % 4, m:m + 1]
                    if v == 0 and n == 1:
                        ins = dve.tensor_scalar(dst, src, x, None, ALU.mult)
                    else:
                        if n == 1:
                            dve.wait_ge(dve_read, i * (NV * D) + (NV * t + v + DVE_CREDIT))
                        elif v or n:
                            dve.wait_ge(mac_done, i * (3 * NV * D) + (3 * NV * t + 3 * v + max(n - 1, 0)))
                        first = b2_row[:, :] if v == 0 and n == 0 else dst
                        ins = dve.scalar_tensor_tensor(out=dst, in0=src, scalar=x, in1=first,
                                                       op0=ALU.mult, op1=ALU.add)
                    if n < 3:
                        ins.then_inc(mac_done, 1)
                    else:
                        ins.then_inc(dve_read, 1)

            def fold(i, t, step):
                mine = scaled[:, t % 2]
                done = NA * t + ACT_CREDIT
                if step:
                    dve.wait_ge(fold_step, i * (7 * D) + (7 * t + step))
                if step == 0:
                    dve.wait_ge(act_scaled, i * (NA * D) + (done + 4))
                    dve.tensor_tensor(fold4[:, :], mine[:, 2, :], mine[:, 3, :], ALU.add).then_inc(fold_step, 1)
                elif step == 1:
                    dve.wait_ge(act_scaled, i * (NA * D) + (done + 5))
                    dve.tensor_tensor(fold4[:, :], fold4[:, :], mine[:, 4, :], ALU.add).then_inc(fold_step, 1)
                elif step == 2:
                    n = S * len(fields(NG - 1))
                    dve.wait_ge(act_scaled, i * (NA * D) + (done + 6))
                    dve.tensor_tensor(fold4[:, 0:n], fold4[:, 0:n], mine[:, 5, 0:n], ALU.add).then_inc(fold_step, 1)
                elif step == 3:
                    dve.wait_ge(pool_added, i * D + (t + 1))
                    dve.tensor_tensor(fold4[:, :], fold4[:, :], pool_sum[:, t % 2, :], ALU.add).then_inc(fold_step, 1)
                elif step == 4:
                    dve.tensor_tensor(fold2[:, :], fold4[:, 0:2 * S], fold4[:, 2 * S:4 * S], ALU.add).then_inc(fold_step, 1)
                elif step == 5:
                    dve.wait_ge(dve_read, i * (NV * D) + (NV * t + NV + DVE_CREDIT))
                    dve.tensor_tensor(fold2[:, :], fold2[:, :], mac[:, t % 2, :], ALU.add).then_inc(fold_step, 1)
                elif step == 6:
                    dve.tensor_tensor(fold1[:, :], fold2[:, 0:S], fold2[:, S:2 * S], ALU.add).then_inc(fold_step, 1)
                elif t == 0:
                    dve.tensor_scalar(p2_part[:, :], fold1[:, :], 0.0, None, ALU.max).then_inc(folded, 1)
                else:
                    dve.wait_ge(folded, i * D + (t + FOLD_CREDIT))
                    dst = p2_part[:, :] if t < D - 1 else p2_all[:, bass.ds(i * S, S)]
                    dve.scalar_tensor_tensor(out=dst, in0=fold1[:, :], scalar=0.0, in1=p2_part[:, :],
                                             op0=ALU.max, op1=ALU.add).then_inc(folded, 1)

            def stage(g):
                src = emb[:, :].rearrange("p (m d) -> p d m", d=D)[:, 4 * g:4 * g + 4, :]
                dve.tensor_copy(x0[:, g, :, 0:M], src).then_inc(staged, 1)
                dve.tensor_copy(x0[:, g, :, M:EXT], src[:, :, 0:EXT - M]).then_inc(staged, 1)

            def low_part(i, pair):
                i, pair = (i + 1, pair - D // 2) if pair >= D // 2 else (i, pair)
                dve.wait_ge(x1_rounded, i * (D // 2) + (pair + 1))
                full = x1_full[:, 2 * pair:2 * pair + 2, :].rearrange("p d n -> p (d n)")
                dve.tensor_tensor(x1_low[:, pair % 2, :], full, x1_high[:, pair % 2, :].bitcast(F32),
                                  ALU.subtract).then_inc(x1_split, 1)

            def body(i, last=False):
                stage(3)
                for t in range(D):
                    for step in range(8):
                        if not (last and t == D - 1):
                            macs(i, t + 1, step // 2, step % 2)
                        fold(i, t, step)
                        if step == 5 and t % 2 == 0 and not (last and t == D - 2):
                            low_part(i, t // 2 + 1)
                    if not last and 10 <= t <= 12:
                        if t == 10:
                            dve.wait_ge(gathered, i * (16 * M) + 32 * M)
                        stage(t - 10)
                    if t == D - 3:
                        dve.tensor_reduce(p1_all[:, bass.ds(i * P, P)], x1_full[:, :, :].rearrange("p d n -> p n d"),
                                          AX_X, ALU.add).then_inc(p1_reduced, 1)

            dve.sem_inc(dve_read, DVE_CREDIT)
            dve.sem_inc(folded, FOLD_CREDIT)
            dve.memset(pairs[:, :, PAIRS:CH * CK], 0.0).then_inc(w1_step, 1)
            dve.memset(w1_fold[:, PAIRS:CH * CK], 0.0).then_inc(w1_step, 1)
            dve.wait_ge(w1_in, 16)
            W = EXT - M
            dve.tensor_copy(w1_ext[:, 0:M, M:EXT], w1_ext[:, 0:M, 0:W]).then_inc(w1_step, 1)
            dve.tensor_copy(w1_ext[:, M:EXT, 0:M], w1_ext[:, 0:W, 0:M]).then_inc(w1_step, 1)
            flat = w1_ext[:, 0, 0:M]
            part = list(flat.ap[0])
            over = bass.AP(flat.tensor, flat.offset + 1, [part, [1, SHIFTS - 1], [EXT + 1, M]])
            under = bass.AP(flat.tensor, flat.offset + EXT, [part, [EXT, SHIFTS - 1], [EXT + 1, M]])
            diag = bass.AP(flat.tensor, flat.offset, [part, [EXT + 1, M]])
            dve.tensor_copy(w1_fold[:, 0:M], diag).then_inc(w1_step, 1)
            dve.wait_ge(w1_step, 4)
            dve.tensor_tensor(w1_fold[:, M:PAIRS].rearrange("p (k h) -> p k h", h=M), over, under,
                              ALU.add).then_inc(w1_step, 1)
            dve.wait_ge(small_in, SMALL)
            for q in range(NG):
                dve.wait_ge(w2_rounded, q + 1)
                n = S * len(fields(q))
                cols = slice(MB * S * q, MB * S * q + n)
                dve.tensor_tensor(w2_low[:, cols], y_bank[:, q % RING, 0:n], w2_high[:, cols].bitcast(F32),
                                  ALU.subtract).then_inc(w2_split, 1)
            dve.wait_ge(gathered, 16 * M)
            for g in range(3):
                stage(g)
            low_part(0, 0)
            for step in range(8):
                macs(0, 0, step // 2, step % 2)
            with dve.Fori(0, NB - 1, 1) as i:
                body(i)
            body(NB - 1, last=True)


_TABLES = [f"tbl_{n}" for n in range(39)]
_INS = (["dense_ctx", "ids"] + _TABLES + ["W_top1", "b_top1", "W_top2", "b_top2", "W_top3",
        "L0_rec_W1", "L0_rec_b1", "L0_rec_W2", "L0_rec_b2"])


def kernel(**inputs):
    import numpy as _np
    import concourse.bacc as _bacc
    from concourse import mybir as _mybir
    from concourse.bass_utils import run_bass_kernel_spmd as _run

    nc = _bacc.Bacc("TRN2", target_bir_lowering=False, num_devices=1)
    arrays, aps = {}, {}
    for name in _INS + ["identity"]:
        a = _np.eye(128, dtype=_np.float32) if name == "identity" else _np.ascontiguousarray(inputs[name])
        arrays[f"in_{name}"] = a
        aps[name] = nc.dram_tensor(f"in_{name}", a.shape, _mybir.dt.from_np(a.dtype), kind="ExternalInput").ap()
    rows = inputs["ids"].shape[0]
    out = nc.dram_tensor("out_y", (rows, 1), _mybir.dt.float32, kind="ExternalOutput").ap()
    ids = aps["ids"].bitcast(_mybir.dt.uint32)
    build(nc, aps["dense_ctx"], ids, [aps[n] for n in _TABLES], aps["W_top1"], aps["b_top1"], aps["W_top2"],
          aps["b_top2"], aps["W_top3"], aps["L0_rec_W1"], aps["L0_rec_b1"], aps["L0_rec_W2"], aps["L0_rec_b2"],
          aps["identity"], out)
    r = _run(nc, [arrays], core_ids=[0])
    return r.results[0]["out_y"]
```

```python
from contextlib import ExitStack

import concourse.bass as bass
from concourse import mybir

F32 = mybir.dt.float32
F32R = mybir.dt.float32r
U32 = mybir.dt.uint32
ALU = mybir.AluOpType
ACT = mybir.ActivationFunctionType
AX_X = mybir.AxisListType.X

P = 128
D = 16
BANK = 512
MB = BANK // P
RING = 5
DVE_BANKS = (2, 5, 8)
ACT_CREDIT = 4
DVE_CREDIT = 3
FOLD_CREDIT = 2
PREP = 4


def build(nc, dense_ctx, ids, tables, W_top1, b_top1, W_top2, b_top2, W_top3, W1, b1, W2, b2, eye, out):
    B, DC = dense_ctx.shape
    S, M, _ = W1.shape
    NB = B // P
    SHIFTS = (M + 1) // 2
    PAIRS = SHIFTS * M
    CH = 7
    CK = (PAIRS + CH - 1) // CH
    EXT = M + SHIFTS - 1
    NG = (M + MB - 1) // MB
    H1, H2 = W_top1.shape[1], W_top2.shape[1]
    dve_banks = list(DVE_BANKS)
    act_banks = [q for q in range(NG) if q not in dve_banks]
    NA, NV = len(act_banks), len(dve_banks)
    assert (S, NG, NA, NV, D) == (P, 2 * RING, 7, 3, 16)

    GATHER = range(1, 11)
    BRIEF = (4, 8)

    def pool_banks(t):
        return 2 if t in BRIEF else 3 if t in GATHER else 4

    def pool_steps(t):
        return sum(pool_banks(n) - 1 for n in range(t))

    def fold_steps(t):
        return sum(NA - pool_banks(n) + 3 for n in range(t))

    def fields(q):
        return range(MB * q, min(MB * q + MB, M))

    with ExitStack() as ctx:
        def sb(name, shape, dt=F32):
            return ctx.enter_context(nc.sbuf_tensor(name, shape, dt))

        def sem(name):
            return ctx.enter_context(nc.semaphore(name))

        y_bank = ctx.enter_context(nc.psum_tensor("y_bank", [P, RING, BANK], F32))
        turn_bank = ctx.enter_context(nc.psum_tensor("turn_bank", [P, 2, BANK], F32))
        x1_bank = ctx.enter_context(nc.psum_tensor("x1_bank", [P, BANK], F32))

        ident = sb("ident", [P, P])
        idx = sb("idx", [P, M], U32)
        emb = sb("emb", [P, M * D])
        x0 = sb("x0", [P, D // 4, 4, EXT])
        pairs = sb("pairs", [P, 2, CH * CK])
        pairs_high = sb("pairs_high", [P, 2, CH, 2 * P], F32R)
        pairs_low = sb("pairs_low", [P, 2, CH, 2 * P], F32R)
        w1_ext = sb("w1_ext", [P, EXT, EXT])
        w1_fold = sb("w1_fold", [P, CH * CK])
        w1_high = sb("w1_high", [P, CH, S], F32R)
        w1_low = sb("w1_low", [P, CH, S], F32R)
        w2_flat = sb("w2_flat", [P, P * M])
        w2_raw = w2_flat[:, :].rearrange("p (h m) -> p h m", m=M)
        w2_high = sb("w2_high", [P, M * S], F32R)
        w2_low = sb("w2_low", [P, M * S], F32R)
        b1_col = sb("b1_col", [P, 1])
        gate = sb("gate", [P, 1])
        b2_row = sb("b2_row", [P, S])
        x1_full = sb("x1_full", [P, D, P])
        x1_high = sb("x1_high", [P, 2, 2 * P], F32R)
        x1_low = sb("x1_low", [P, 2, 2 * P], F32R)
        scaled = sb("scaled", [P, 2, NA, BANK])
        pool_sum = sb("pool_sum", [P, 2, BANK])
        mac = sb("mac", [P, 2, 2 * S])
        fold4 = sb("fold4", [P, BANK])
        fold2 = sb("fold2", [P, 2 * S])
        fold1 = sb("fold1", [P, S])
        p2_part = sb("p2_part", [P, S])
        p1_all = sb("p1_all", [P, B])
        p2_all = sb("p2_all", [P, NB * S])
        p2_t = sb("p2_t", [P, B])
        dense = sb("dense", [P, NB, DC])
        dense_t = sb("dense_t", [P, B])
        wt1 = sb("wt1", [P, 3, H1])
        wt2 = sb("wt2", [P, H1 // P, H2])
        wt3 = sb("wt3", [P, H2 // P])
        bt1 = sb("bt1", [P, H1 // P])
        bt2 = sb("bt2", [P, H2 // P])
        h1 = w2_flat[:, 0:H1 // P * BANK].rearrange("p (c n) -> p c n", n=BANK)
        h2 = w2_flat[:, H1 // P * BANK:(H1 + H2) // P * BANK].rearrange("p (c n) -> p c n", n=BANK)
        y_row = sb("y_row", [1, B])

        ids_in = sem("ids_in")
        ident_in = sem("ident_in")
        w1_in = sem("w1_in")
        w2_in = sem("w2_in")
        small_in = sem("small_in")
        gathered = sem("gathered")
        w1_step = sem("w1_step")
        w1_turned = sem("w1_turned")
        w1_rounded = sem("w1_rounded")
        w1_split = sem("w1_split")
        w2_turned = sem("w2_turned")
        w2_rounded = sem("w2_rounded")
        w2_split = sem("w2_split")
        dense_turned = sem("dense_turned")
        dense_copied = sem("dense_copied")
        staged = sem("staged")
        paired = sem("paired")
        turned = sem("turned")
        pairs_rounded = sem("pairs_rounded")
        pairs_split = sem("pairs_split")
        l1_done = sem("l1_done")
        x1_rounded = sem("x1_rounded")
        x1_split = sem("x1_split")
        y_for_act = sem("y_for_act")
        y_for_dve = sem("y_for_dve")
        act_scaled = sem("act_scaled")
        mac_done = sem("mac_done")
        dve_read = sem("dve_read")
        pool_added = sem("pool_added")
        fold_step = sem("fold_step")
        folded = sem("folded")
        p1_reduced = sem("p1_reduced")
        p2_turned = sem("p2_turned")
        p2_copied = sem("p2_copied")
        top_sum = sem("top_sum")
        top_act = sem("top_act")
        y_out = sem("y_out")

        block = ctx.enter_context(nc.Block())

        @block.sync
        def _(sp):
            sp.dma_start(idx[:, :], ids[0:P, :]).then_inc(ids_in, 16)
            sp.dma_start(w1_ext[:, 0:M, 0:M], W1).then_inc(w1_in, 16)
            sp.dma_start(ident[:, :], eye).then_inc(ident_in, 16)
            sp.dma_start(w2_raw[:, :, :], W2).then_inc(w2_in, 16)
            small = [
                (b1_col[:, :], b1.rearrange("(s o) -> s o", o=1)),
                (b2_row[:, :], b2.rearrange("(o s) -> o s", o=1).to_broadcast([P, S])),
                (dense[:, :, :], dense_ctx.rearrange("(t p) c -> p t c", p=P)),
                (wt1[:, 0:2, :], W_top1[0:2 * P, :].rearrange("(c p) n -> p c n", p=P)),
                (wt1[0:DC, 2, :], W_top1[2 * P:2 * P + DC, :]),
                (wt2[:, :, :], W_top2.rearrange("(c p) n -> p c n", p=P)),
                (wt3[:, :], W_top3.rearrange("(c p) o -> p (c o)", p=P)),
                (bt1[:, :], b_top1.rearrange("(c p) -> p c", p=P)),
                (bt2[:, :], b_top2.rearrange("(c p) -> p c", p=P)),
            ]
            with nc.allow_non_contiguous_dma(reason="a few hundred bias and W_top3 elements"):
                for dst, src in small:
                    sp.dma_start(dst, src).then_inc(small_in, 16)
            with sp.Fori(0, NB - 1, 1) as i:
                sp.wait_ge(gathered, i * (16 * M) + 16 * M)
                sp.dma_start(idx[:, :], ids[bass.ds(i * P + P, P), :]).then_inc(ids_in, 16)
            sp.wait_ge(top_act, 2 * (H1 // P + H2 // P + 1))
            sp.dma_start(out.rearrange("b o -> o b"), y_row[:, :]).then_inc(y_out, 16)
            sp.wait_ge(y_out, 16)
        SMALL = 16 * 9

        @block.gpsimd
        def _(pool):
            def gather(f):
                pool.indirect_dma_start(emb[:, f * D:(f + 1) * D], None, tables[f],
                                        bass.IndirectOffsetOnAxis(ap=idx[:, f:f + 1], axis=0)).then_inc(gathered, 16)

            def products(i, t):
                i, t = (i + 1, t - D) if t >= D else (i, t)
                g, dd = t // 4, t % 4
                pool.wait_ge(staged, i * 8 + (2 * g + 2))
                if not (isinstance(i, int) and i == 0 and t < 2):
                    pool.wait_ge(turned, i * (2 * D) + (2 * t - 2))
                base = x0[:, g, dd, 0:M]
                near = base.unsqueeze(1).to_broadcast([P, SHIFTS, M])
                far = bass.AP(base.tensor, base.offset, [list(base.ap[0]), [1, SHIFTS], [1, M]])
                dst = pairs[:, t % 2, 0:PAIRS].rearrange("p (k h) -> p k h", h=M)
                pool.tensor_tensor(dst, near, far, ALU.mult).then_inc(paired, 1)

            def add_banks(i, t):
                mine = scaled[:, t % 2]
                dst = pool_sum[:, t % 2, :]
                pool.wait_ge(folded, i * D + (t - 1 + FOLD_CREDIT))
                pool.wait_ge(act_scaled, i * (NA * D) + (NA * t + 2 + ACT_CREDIT))
                pool.tensor_tensor(dst, mine[:, 0, :], mine[:, 1, :], ALU.add).then_inc(pool_added, 1)
                for n in range(2, pool_banks(t)):
                    pool.wait_ge(act_scaled, i * (NA * D) + (NA * t + n + 1 + ACT_CREDIT))
                    pool.wait_ge(pool_added, i * pool_steps(D) + (pool_steps(t) + n - 1))
                    pool.tensor_tensor(dst, dst, mine[:, n, :], ALU.add).then_inc(pool_added, 1)

            def gathers(t):
                n = t - GATHER[0]
                for f in range(M * n // len(GATHER), M * (n + 1) // len(GATHER)):
                    gather(f)

            def body(i, last=False):
                for t in range(D):
                    if not (last and t + PREP >= D):
                        products(i, t + PREP)
                    if not last and t == GATHER[0]:
                        pool.wait_ge(staged, i * 8 + 8)
                        pool.wait_ge(ids_in, i * 16 + 32)
                        pool.tensor_tensor(gate[:, :], b1_col[:, :], b1_col[:, :], ALU.add)
                    if not last and t in GATHER:
                        gathers(t)
                    add_banks(i, t)

            pool.wait_ge(ids_in, 16)
            for f in range(M):
                gather(f)
            pool.wait_ge(small_in, SMALL)
            pool.wait_ge(w1_step, 1)
            for t in range(PREP):
                products(0, t)
            with pool.Fori(0, NB - 1, 1) as i:
                body(i)
            body(NB - 1, last=True)

        @block.tensor
        def _(pe):
            def turn(i, t, half):
                i, t = (i + 1, t - D) if t >= D else (i, t)
                if half == 0:
                    pe.wait_ge(paired, i * D + (t + 1))
                if not (isinstance(i, int) and i == 0 and t == 0):
                    pe.wait_ge(pairs_split, i * (2 * D) + (2 * t - 1 + half))
                chunks = range(0, 4) if half == 0 else range(4, CH)
                for n, c in enumerate(chunks):
                    mm = pe.transpose(turn_bank[0:CK, half, n * P:(n + 1) * P],
                                      pairs[:, t % 2, c * CK:(c + 1) * CK], ident[:, :])
                mm.then_inc(turned, 1)

            def layer1(i, pair, c):
                i, pair = (i + 1, pair - D // 2) if pair >= D // 2 else (i, pair)
                if c == 0:
                    pe.wait_ge(pairs_split, i * (2 * D) + (4 * pair + 4))
                    if not (isinstance(i, int) and i == 0 and pair == 0):
                        pe.wait_ge(x1_rounded, i * (D // 2) + pair)
                dst = x1_bank[:, 0:2 * P]
                high, low = pairs_high[0:CK, pair % 2, c, :], pairs_low[0:CK, pair % 2, c, :]
                pe.matmul(dst, w1_low[0:CK, c, :], high, start=(c == 0), stop=False)
                pe.matmul(dst, w1_high[0:CK, c, :], low, start=False, stop=False)
                mm = pe.matmul(dst, w1_high[0:CK, c, :], high, start=False, stop=(c == CH - 1))
                if c == CH - 1:
                    mm.then_inc(l1_done, 1)

            def layer2(i, t, q):
                bank, n = q % RING, S * len(fields(q))
                if q == 0 and t % 2 == 0:
                    pe.wait_ge(x1_split, i * (D // 2) + (t // 2 + 1))
                before, n_t = (q - RING, t) if q >= RING else (q + RING, t - 1)
                if before in act_banks:
                    pe.wait_ge(act_scaled, i * (NA * D) + (NA * n_t + act_banks.index(before) + 1 + ACT_CREDIT))
                else:
                    pe.wait_ge(dve_read, i * (NV * D) + (NV * n_t + dve_banks.index(before) + 1 + DVE_CREDIT))
                cols = slice(MB * S * q, MB * S * q + n)
                high = x1_high[:, t // 2 % 2, t % 2 * P:(t % 2 + 1) * P]
                low = x1_low[:, t // 2 % 2, t % 2 * P:(t % 2 + 1) * P]
                dst = y_bank[:, bank, 0:n]
                pe.matmul(dst, low, w2_high[:, cols], start=True, stop=False)
                pe.matmul(dst, high, w2_low[:, cols], start=False, stop=False)
                mm = pe.matmul(dst, high, w2_high[:, cols], start=False, stop=True)
                mm.then_inc(y_for_act if q in act_banks else y_for_dve, 1)

            BEHIND = [
                {2: ("turn", 0), 4: ("l1", 0), 5: ("turn", 1), 6: ("l1", 1), 7: ("l1", 2), 9: ("l1", 3)},
                {0: ("l1", 4), 1: ("turn", 0), 2: ("l1", 5), 3: ("l1", 6), 5: ("turn", 1)},
            ]

            def body(i, last=False):
                for t in range(D):
                    for q in range(NG):
                        layer2(i, t, q)
                        what, n = BEHIND[t % 2].get(q, (None, 0))
                        if what == "l1" and not (last and t // 2 + 1 >= D // 2):
                            layer1(i, t // 2 + 1, n)
                        if what == "turn" and not (last and t + PREP >= D):
                            turn(i, t + PREP, n)

            pe.wait_ge(ident_in, 16)
            pe.wait_ge(w2_in, 16)
            for q in range(NG):
                if q >= RING:
                    pe.wait_ge(w2_split, q - RING + 1)
                for n, m in enumerate(fields(q)):
                    mm = pe.transpose(y_bank[:, q % RING, n * P:(n + 1) * P], w2_raw[:, :, m], ident[:, :])
                mm.then_inc(w2_turned, 1)
            pe.wait_ge(w1_step, 6)
            for c in range(CH):
                mm = pe.transpose(turn_bank[0:CK, c // 4, c % 4 * P:(c % 4 + 1) * P],
                                  w1_fold[:, c * CK:(c + 1) * CK], ident[:, :])
            mm.then_inc(w1_turned, 1)
            pe.wait_ge(small_in, SMALL)
            for half in range(2):
                if half:
                    pe.wait_ge(dense_copied, 1)
                for n in range(NB // 2):
                    mm = pe.transpose(x1_bank[0:DC, n * P:(n + 1) * P], dense[:, half * NB // 2 + n, :], ident[:, :])
                mm.then_inc(dense_turned, 1)
            pe.wait_ge(w1_split, 2)
            for t in range(PREP):
                turn(0, t, 0)
                turn(0, t, 1)
            pe.wait_ge(dense_copied, 2)
            for c in range(CH):
                layer1(0, 0, c)
            pe.wait_ge(w2_split, NG)
            with pe.Fori(0, NB - 1, 1) as i:
                body(i)
            body(NB - 1, last=True)

            pe.wait_ge(folded, NB * D + FOLD_CREDIT)
            for half in range(2):
                for n in range(NB // 2):
                    b = half * NB // 2 + n
                    mm = pe.transpose(turn_bank[:, half, n * P:(n + 1) * P], p2_all[:, b * S:(b + 1) * S], ident[:, :])
                mm.then_inc(p2_turned, 1)
            pe.wait_ge(p1_reduced, 4 * NB)
            pe.wait_ge(act_scaled, NB * NA * D + ACT_CREDIT)
            step = 0
            for half in range(2):
                rows = slice(half * BANK, (half + 1) * BANK)
                pe.wait_ge(p2_copied, half + 1)
                for c in range(H1 // P):
                    if step >= RING:
                        pe.wait_ge(top_act, step - RING + 1)
                    dst = y_bank[:, step % RING, :]
                    cols = slice(c * P, (c + 1) * P)
                    pe.matmul(dst, wt1[:, 0, cols], p1_all[:, rows], start=True, stop=False)
                    pe.matmul(dst, wt1[0:DC, 2, cols], dense_t[0:DC, rows], start=False, stop=False)
                    pe.matmul(dst, wt1[:, 1, cols], p2_t[:, rows], start=False, stop=True).then_inc(top_sum, 1)
                    step += 1
                pe.wait_ge(top_act, step)
                for c in range(H2 // P):
                    for k in range(H1 // P):
                        mm = pe.matmul(y_bank[:, step % RING, :], wt2[:, k, c * P:(c + 1) * P], h1[:, k, :],
                                       start=(k == 0), stop=(k == H1 // P - 1))
                    mm.then_inc(top_sum, 1)
                    step += 1
                pe.wait_ge(top_act, step)
                for k in range(H2 // P):
                    mm = pe.matmul(y_bank[0:1, step % RING, :], wt3[:, k:k + 1], h2[:, k, :],
                                   start=(k == 0), stop=(k == H2 // P - 1))
                mm.then_inc(top_sum, 1)
                step += 1

        @block.scalar
        def _(act):
            def scale(i, t, a):
                q = act_banks[a]
                if a == 0:
                    act.wait_ge(folded, i * D + (t - 1 + FOLD_CREDIT))
                act.wait_ge(y_for_act, i * (NA * D) + (NA * t + a + 1))
                for n, m in enumerate(fields(q)):
                    ins = act.activation(scaled[:, t % 2, a, n * S:(n + 1) * S], y_bank[:, q % RING, n * S:(n + 1) * S],
                                         ACT.Copy, scale=x0[:, t // 4, t % 4, m:m + 1])
                ins.then_inc(act_scaled, 1)

            def pairs_to_high(i, t, half):
                i, t = (i + 1, t - D) if t >= D else (i, t)
                act.wait_ge(turned, i * (2 * D) + (2 * t + half + 1))
                if t % 2 == 0 and half == 0 and not (isinstance(i, int) and i == 0 and t < 4):
                    act.wait_ge(l1_done, i * (D // 2) + (t // 2 - 1))
                c0, c1 = (0, 4) if half == 0 else (4, CH)
                act.activation(pairs_high[0:CK, t // 2 % 2, c0:c1, t % 2 * P:(t % 2 + 1) * P],
                               turn_bank[0:CK, half, 0:(c1 - c0) * P].rearrange("p (c n) -> p c n", n=P),
                               ACT.Copy).then_inc(pairs_rounded, 1)

            def first_maps(i, pair):
                i, pair = (i + 1, pair - D // 2) if pair >= D // 2 else (i, pair)
                act.wait_ge(l1_done, i * (D // 2) + (pair + 1))
                if pair == 0 and not (isinstance(i, int) and i == 0):
                    act.wait_ge(p1_reduced, i * 4)
                act.activation(x1_full[:, 2 * pair:2 * pair + 2, :],
                               x1_bank[:, 0:2 * P].rearrange("p (d n) -> p d n", n=P),
                               ACT.Relu, bias=b1_col[:, 0:1])
                act.activation(x1_high[:, pair % 2, :], x1_bank[:, 0:2 * P],
                               ACT.Relu, bias=b1_col[:, 0:1]).then_inc(x1_rounded, 1)

            BEHIND = [
                {1: ("high", 0), 5: ("high", 1)},
                {1: ("high", 0), 3: ("maps", 0), 5: ("high", 1)},
            ]

            def body(i, last=False):
                for t in range(D):
                    for a in range(NA):
                        scale(i, t, a)
                        what, n = BEHIND[t % 2].get(a, (None, 0))
                        if what == "maps" and not (last and t // 2 + 1 >= D // 2):
                            first_maps(i, t // 2 + 1)
                        if what == "high" and not (last and t + PREP >= D):
                            pairs_to_high(i, t + PREP, n)

            act.sem_inc(act_scaled, ACT_CREDIT)
            for q in range(NG):
                act.wait_ge(w2_turned, q + 1)
                n = S * len(fields(q))
                act.activation(w2_high[:, MB * S * q:MB * S * q + n], y_bank[:, q % RING, 0:n],
                               ACT.Copy).then_inc(w2_rounded, 1)
            act.wait_ge(w1_turned, 1)
            for half, (c0, c1) in enumerate([(0, 4), (4, CH)]):
                src = turn_bank[0:CK, half, 0:(c1 - c0) * P].rearrange("p (c n) -> p c n", n=P)
                act.activation(w1_high[0:CK, c0:c1, :], src, ACT.Copy).then_inc(w1_rounded, 1)
            act.wait_ge(small_in, SMALL)
            for half in range(2):
                act.wait_ge(dense_turned, half + 1)
                act.activation(dense_t[0:DC, half * BANK:(half + 1) * BANK], x1_bank[0:DC, :],
                               ACT.Copy).then_inc(dense_copied, 1)
            for t in range(PREP):
                pairs_to_high(0, t, 0)
                pairs_to_high(0, t, 1)
            first_maps(0, 0)
            with act.Fori(0, NB - 1, 1) as i:
                body(i)
            body(NB - 1, last=True)

            for half in range(2):
                act.wait_ge(p2_turned, half + 1)
                act.activation(p2_t[:, half * BANK:(half + 1) * BANK], turn_bank[:, half, :],
                               ACT.Copy).then_inc(p2_copied, 1)
            step = 0
            for half in range(2):
                for c in range(H1 // P):
                    act.wait_ge(top_sum, step + 1)
                    act.activation(h1[:, c, :], y_bank[:, step % RING, :], ACT.Relu,
                                   bias=bt1[:, c:c + 1]).then_inc(top_act, 1)
                    step += 1
                for c in range(H2 // P):
                    act.wait_ge(top_sum, step + 1)
                    act.activation(h2[:, c, :], y_bank[:, step % RING, :], ACT.Relu,
                                   bias=bt2[:, c:c + 1]).then_inc(top_act, 1)
                    step += 1
                act.wait_ge(top_sum, step + 1)
                act.activation(y_row[:, half * BANK:(half + 1) * BANK], y_bank[0:1, step % RING, :],
                               ACT.Copy).then_inc(top_act, 1)
                step += 1

        @block.vector
        def _(dve):
            def macs(i, t, v, part):
                i, t = (i + 1, t - D) if t >= D else (i, t)
                q = dve_banks[v]
                if part == 0:
                    dve.wait_ge(y_for_dve, i * (NV * D) + (NV * t + v + 1))
                for n in (2 * part, 2 * part + 1):
                    m = MB * q + n
                    src = y_bank[:, q % RING, n * S:(n + 1) * S]
                    dst = mac[:, t % 2, n % 2 * S:(n % 2 + 1) * S]
                    x = x0[:, t // 4, t % 4, m:m + 1]
                    if v == 0 and n == 1:
                        ins = dve.tensor_scalar(dst, src, x, None, ALU.mult)
                    else:
                        if n == 1:
                            dve.wait_ge(dve_read, i * (NV * D) + (NV * t + v + DVE_CREDIT))
                        elif v or n:
                            dve.wait_ge(mac_done, i * (3 * NV * D) + (3 * NV * t + 3 * v + max(n - 1, 0)))
                        first = b2_row[:, :] if v == 0 and n == 0 else dst
                        ins = dve.scalar_tensor_tensor(out=dst, in0=src, scalar=x, in1=first,
                                                       op0=ALU.mult, op1=ALU.add)
                    if n < 3:
                        ins.then_inc(mac_done, 1)
                    else:
                        ins.then_inc(dve_read, 1)

            def fold(i, t, step):
                mine = scaled[:, t % 2]
                first = pool_banks(t)
                banks = NA - first
                if step > banks + 3:
                    return
                if step:
                    dve.wait_ge(fold_step, i * fold_steps(D) + (fold_steps(t) + step))
                if step == 0:
                    dve.wait_ge(act_scaled, i * (NA * D) + (NA * t + first + 2 + ACT_CREDIT))
                    dve.tensor_tensor(fold4[:, :], mine[:, first, :], mine[:, first + 1, :],
                                      ALU.add).then_inc(fold_step, 1)
                elif step < banks - 1:
                    a = first + 1 + step
                    n = S * len(fields(act_banks[a]))
                    dve.wait_ge(act_scaled, i * (NA * D) + (NA * t + a + 1 + ACT_CREDIT))
                    dve.tensor_tensor(fold4[:, 0:n], fold4[:, 0:n], mine[:, a, 0:n], ALU.add).then_inc(fold_step, 1)
                elif step == banks - 1:
                    dve.wait_ge(pool_added, i * pool_steps(D) + pool_steps(t + 1))
                    dve.tensor_tensor(fold4[:, :], fold4[:, :], pool_sum[:, t % 2, :], ALU.add).then_inc(fold_step, 1)
                elif step == banks:
                    dve.tensor_tensor(fold2[:, :], fold4[:, 0:2 * S], fold4[:, 2 * S:4 * S],
                                      ALU.add).then_inc(fold_step, 1)
                elif step == banks + 1:
                    dve.wait_ge(dve_read, i * (NV * D) + (NV * t + NV + DVE_CREDIT))
                    dve.tensor_tensor(fold2[:, :], fold2[:, :], mac[:, t % 2, :], ALU.add).then_inc(fold_step, 1)
                elif step == banks + 2:
                    dve.tensor_tensor(fold1[:, :], fold2[:, 0:S], fold2[:, S:2 * S], ALU.add).then_inc(fold_step, 1)
                elif t == 0:
                    dve.tensor_scalar(p2_part[:, :], fold1[:, :], 0.0, None, ALU.max).then_inc(folded, 1)
                else:
                    dve.wait_ge(folded, i * D + (t + FOLD_CREDIT))
                    dst = p2_part[:, :] if t < D - 1 else p2_all[:, bass.ds(i * S, S)]
                    dve.scalar_tensor_tensor(out=dst, in0=fold1[:, :], scalar=0.0, in1=p2_part[:, :],
                                             op0=ALU.max, op1=ALU.add).then_inc(folded, 1)

            def pairs_to_low(i, t, half):
                i, t = (i + 1, t - D) if t >= D else (i, t)
                dve.wait_ge(pairs_rounded, i * (2 * D) + (2 * t + half + 1))
                c0, c1 = (0, 4) if half == 0 else (4, CH)
                at = (slice(0, CK), t // 2 % 2, slice(c0, c1), slice(t % 2 * P, (t % 2 + 1) * P))
                src = turn_bank[0:CK, half, 0:(c1 - c0) * P].rearrange("p (c n) -> p c n", n=P)
                dve.tensor_tensor(pairs_low[at], src, pairs_high[at].bitcast(F32), ALU.subtract).then_inc(pairs_split, 1)

            def sum_p1(i, part):
                n = P // 4
                ins = dve.tensor_reduce(p1_all[:, bass.ds(i * P + part * n, n)],
                                        x1_full[:, :, part * n:(part + 1) * n].rearrange("p d n -> p n d"),
                                        AX_X, ALU.add)
                ins.then_inc(p1_reduced, 1)

            def stage(g):
                src = emb[:, :].rearrange("p (m d) -> p d m", d=D)[:, 4 * g:4 * g + 4, :]
                dve.tensor_copy(x0[:, g, :, 0:M], src).then_inc(staged, 1)
                dve.tensor_copy(x0[:, g, :, M:EXT], src[:, :, 0:EXT - M]).then_inc(staged, 1)

            def low_part(i, pair):
                i, pair = (i + 1, pair - D // 2) if pair >= D // 2 else (i, pair)
                dve.wait_ge(x1_rounded, i * (D // 2) + (pair + 1))
                full = x1_full[:, 2 * pair:2 * pair + 2, :].rearrange("p d n -> p (d n)")
                dve.tensor_tensor(x1_low[:, pair % 2, :], full, x1_high[:, pair % 2, :].bitcast(F32),
                                  ALU.subtract).then_inc(x1_split, 1)

            ORDER = [
                [("fold", 0), ("low", 1), ("fold", 1), ("mac", 0, 0), ("fold", 2), ("mac", 0, 1), ("fold", 3),
                 ("low", 0), ("mac", 1, 0), ("fold", 4), ("mac", 1, 1), ("stage",), ("x1",), ("p1", 0),
                 ("fold", 5), ("mac", 2, 0), ("fold", 6), ("mac", 2, 1), ("fold", 7), ("fold", 8), ("p1", 1)],
                [("fold", 0), ("low", 1), ("fold", 1), ("mac", 0, 0), ("fold", 2), ("mac", 0, 1), ("fold", 3),
                 ("low", 0), ("mac", 1, 0), ("fold", 4), ("mac", 1, 1), ("stage",), ("p1", 0),
                 ("fold", 5), ("mac", 2, 0), ("fold", 6), ("mac", 2, 1), ("fold", 7), ("fold", 8), ("p1", 1)],
            ]
            STAGE = {10: 0, 11: 1, 12: 2}
            P1 = {(D - 4, 0): 0, (D - 4, 1): 1, (D - 3, 0): 2, (D - 3, 1): 3}

            def body(i, last=False):
                stage(3)
                for t in range(D):
                    for what, *n in ORDER[t % 2]:
                        if what == "mac" and not (last and t == D - 1):
                            macs(i, t + 1, *n)
                        if what == "fold":
                            fold(i, t, *n)
                        if what == "low":
                            ahead = t + PREP + (1 - n[0])
                            if not (last and ahead >= D):
                                pairs_to_low(i, ahead, *n)
                        if what == "x1" and not (last and t == D - 2):
                            low_part(i, t // 2 + 1)
                        if what == "p1" and (t, *n) in P1:
                            sum_p1(i, P1[(t, *n)])
                        if what == "stage" and not last and t in STAGE:
                            if STAGE[t] == 0:
                                dve.wait_ge(gathered, i * (16 * M) + 32 * M)
                            stage(STAGE[t])

            dve.sem_inc(dve_read, DVE_CREDIT)
            dve.sem_inc(folded, FOLD_CREDIT)
            dve.memset(pairs[:, :, PAIRS:CH * CK], 0.0).then_inc(w1_step, 1)
            dve.memset(w1_fold[:, PAIRS:CH * CK], 0.0).then_inc(w1_step, 1)
            dve.wait_ge(w1_in, 16)
            W = EXT - M
            dve.tensor_copy(w1_ext[:, 0:M, M:EXT], w1_ext[:, 0:M, 0:W]).then_inc(w1_step, 1)
            dve.tensor_copy(w1_ext[:, M:EXT, 0:M], w1_ext[:, 0:W, 0:M]).then_inc(w1_step, 1)
            flat = w1_ext[:, 0, 0:M]
            part = list(flat.ap[0])
            over = bass.AP(flat.tensor, flat.offset + 1, [part, [1, SHIFTS - 1], [EXT + 1, M]])
            under = bass.AP(flat.tensor, flat.offset + EXT, [part, [EXT, SHIFTS - 1], [EXT + 1, M]])
            diag = bass.AP(flat.tensor, flat.offset, [part, [EXT + 1, M]])
            dve.tensor_copy(w1_fold[:, 0:M], diag).then_inc(w1_step, 1)
            dve.wait_ge(w1_step, 4)
            dve.tensor_tensor(w1_fold[:, M:PAIRS].rearrange("p (k h) -> p k h", h=M), over, under,
                              ALU.add).then_inc(w1_step, 1)
            dve.wait_ge(small_in, SMALL)
            for q in range(NG):
                dve.wait_ge(w2_rounded, q + 1)
                n = S * len(fields(q))
                cols = slice(MB * S * q, MB * S * q + n)
                dve.tensor_tensor(w2_low[:, cols], y_bank[:, q % RING, 0:n], w2_high[:, cols].bitcast(F32),
                                  ALU.subtract).then_inc(w2_split, 1)
            for half, (c0, c1) in enumerate([(0, 4), (4, CH)]):
                dve.wait_ge(w1_rounded, half + 1)
                src = turn_bank[0:CK, half, 0:(c1 - c0) * P].rearrange("p (c n) -> p c n", n=P)
                dve.tensor_tensor(w1_low[0:CK, c0:c1, :], src, w1_high[0:CK, c0:c1, :].bitcast(F32),
                                  ALU.subtract).then_inc(w1_split, 1)
            dve.wait_ge(gathered, 16 * M)
            for g in range(3):
                stage(g)
            for t in range(PREP):
                pairs_to_low(0, t, 0)
                pairs_to_low(0, t, 1)
            low_part(0, 0)
            for v in range(NV):
                macs(0, 0, v, 0)
                macs(0, 0, v, 1)
                if v == 1:
                    pairs_to_low(0, PREP, 0)
            with dve.Fori(0, NB - 1, 1) as i:
                body(i)
            body(NB - 1, last=True)


_TABLES = [f"tbl_{n}" for n in range(39)]
_INS = (["dense_ctx", "ids"] + _TABLES + ["W_top1", "b_top1", "W_top2", "b_top2", "W_top3",
        "L0_rec_W1", "L0_rec_b1", "L0_rec_W2", "L0_rec_b2"])


def kernel(**inputs):
    import numpy as _np
    import concourse.bacc as _bacc
    from concourse import mybir as _mybir
    from concourse.bass_utils import run_bass_kernel_spmd as _run

    nc = _bacc.Bacc("TRN2", target_bir_lowering=False, num_devices=1)
    arrays, aps = {}, {}
    for name in _INS + ["identity"]:
        a = _np.eye(128, dtype=_np.float32) if name == "identity" else _np.ascontiguousarray(inputs[name])
        arrays[f"in_{name}"] = a
        aps[name] = nc.dram_tensor(f"in_{name}", a.shape, _mybir.dt.from_np(a.dtype), kind="ExternalInput").ap()
    rows = inputs["ids"].shape[0]
    out = nc.dram_tensor("out_y", (rows, 1), _mybir.dt.float32, kind="ExternalOutput").ap()
    ids = aps["ids"].bitcast(_mybir.dt.uint32)
    build(nc, aps["dense_ctx"], ids, [aps[n] for n in _TABLES], aps["W_top1"], aps["b_top1"], aps["W_top2"],
          aps["b_top2"], aps["W_top3"], aps["L0_rec_W1"], aps["L0_rec_b1"], aps["L0_rec_W2"], aps["L0_rec_b2"],
          aps["identity"], out)
    r = _run(nc, [arrays], core_ids=[0])
    return r.results[0]["out_y"]
```

```python
from contextlib import ExitStack

import concourse.bass as bass
from concourse import mybir

F32 = mybir.dt.float32
F32R = mybir.dt.float32r
U32 = mybir.dt.uint32
ALU = mybir.AluOpType
ACT = mybir.ActivationFunctionType
AX_X = mybir.AxisListType.X

P = 128
D = 16
BANK = 512
MB = BANK // P
RING = 5
DVE_BANKS = (2, 5, 8)
ACT_CREDIT = 4
DVE_CREDIT = 3
FOLD_CREDIT = 2
PREP = 4


def build(nc, dense_ctx, ids, tables, W_top1, b_top1, W_top2, b_top2, W_top3, W1, b1, W2, b2, eye, out):
    B, DC = dense_ctx.shape
    S, M, _ = W1.shape
    NB = B // P
    SHIFTS = (M + 1) // 2
    PAIRS = SHIFTS * M
    CH = PAIRS // P + 1
    REST = PAIRS % P
    THREE = 96
    LAST = (CH - 1) * P
    EXT = M + SHIFTS - 1
    NG = (M + MB - 1) // MB
    H1, H2 = W_top1.shape[1], W_top2.shape[1]
    dve_banks = list(DVE_BANKS)
    act_banks = [q for q in range(NG) if q not in dve_banks]
    NA, NV = len(act_banks), len(dve_banks)
    assert (S, NG, NA, NV, D) == (P, 2 * RING, 7, 3, 16)

    GATHER = range(1, 12)
    BRIEF = (4,)

    def pool_banks(t):
        return 2 if t in BRIEF else 3 if t in GATHER else 4

    def pool_steps(t):
        return sum(pool_banks(n) - 1 for n in range(t))

    def fold_steps(t):
        return sum(NA - pool_banks(n) + 3 for n in range(t))

    def fields(q):
        return range(MB * q, min(MB * q + MB, M))

    with ExitStack() as ctx:
        def copies(rows):
            return rows[:, LAST + 32:LAST + 96].rearrange("p (r c) -> p r c", c=32)[:, :, 0:REST]

        def form_products(engine, t):
            base = x0[:, t // 4, t % 4, 0:M]
            near = base.unsqueeze(1).to_broadcast([P, SHIFTS, M])
            far = bass.AP(base.tensor, base.offset, [list(base.ap[0]), [1, SHIFTS], [1, M]])
            engine.tensor_tensor(pairs[:, t % 2, 0:PAIRS].rearrange("p (k h) -> p k h", h=M), near, far, ALU.mult)
            near = x0[:, t // 4, t % 4, M - REST:M].unsqueeze(1).to_broadcast([P, 2, REST])
            far = x0[:, t // 4, t % 4, EXT - REST:EXT].unsqueeze(1).to_broadcast([P, 2, REST])
            return engine.tensor_tensor(copies(pairs[:, t % 2, :]), near, far, ALU.mult)

        def landing(i, t, half):
            if isinstance(i, int) and i == 0 and t < 2:
                return y_bank[:, 2 * t + half, :]
            return turn_bank[:, half, :]

        def sb(name, shape, dt=F32):
            return ctx.enter_context(nc.sbuf_tensor(name, shape, dt))

        def sem(name):
            return ctx.enter_context(nc.semaphore(name))

        y_bank = ctx.enter_context(nc.psum_tensor("y_bank", [P, RING, BANK], F32))
        turn_bank = ctx.enter_context(nc.psum_tensor("turn_bank", [P, 2, BANK], F32))
        x1_bank = ctx.enter_context(nc.psum_tensor("x1_bank", [P, BANK], F32))

        ident = sb("ident", [P, P])
        idx = sb("idx", [P, M], U32)
        emb = sb("emb", [P, M * D])
        x0 = sb("x0", [P, D // 4, 4, EXT])
        pairs = sb("pairs", [P, 2, CH * P])
        pairs_high = sb("pairs_high", [P, 2, CH, 2 * P], F32R)
        pairs_low = sb("pairs_low", [P, 2, CH - 1, 2 * P], F32R)
        w1_flat = sb("w1_flat", [P, EXT * EXT])
        w1_ext = w1_flat[:, :].rearrange("p (a b) -> p a b", b=EXT)
        w1_fold = sb("w1_fold", [P, CH * P])
        w1_high = sb("w1_high", [P, CH, S], F32R)
        w1_low = sb("w1_low", [P, CH - 1, S], F32R)
        w2_flat = sb("w2_flat", [P, P * M])
        w2_raw = w2_flat[:, :].rearrange("p (h m) -> p h m", m=M)
        w2_high = sb("w2_high", [P, M * S], F32R)
        w2_low = sb("w2_low", [P, M * S], F32R)
        b1_col = sb("b1_col", [P, 1])
        gate = sb("gate", [P, 1])
        b2_row = sb("b2_row", [P, S])
        x1_full = sb("x1_full", [P, D, P])
        x1_high = sb("x1_high", [P, 2, 2 * P], F32R)
        x1_low = sb("x1_low", [P, 2, 2 * P], F32R)
        scaled = sb("scaled", [P, 2, NA, BANK])
        pool_sum = sb("pool_sum", [P, 2, BANK])
        mac = sb("mac", [P, 2, 2 * S])
        fold4 = sb("fold4", [P, BANK])
        fold2 = sb("fold2", [P, 2 * S])
        fold1 = sb("fold1", [P, S])
        p2_part = sb("p2_part", [P, S])
        p1_all = sb("p1_all", [P, B])
        p2_all = sb("p2_all", [P, NB * S])
        p2_high = sb("p2_high", [P, B], F32R)
        dense_t = sb("dense_t", [THREE, B], F32R)
        wt1_dense = sb("wt1_dense", [THREE, H1], F32R)
        dense = scaled[:, 0, 0:2, :].rearrange("p a (t c) -> p (a t) c", c=P)[:, :, 0:THREE]
        wt1_dense_raw = scaled[0:THREE, 1, 0, 0:H1]
        wt1_high = sb("wt1_high", [P, 2, H1], F32R)
        wt1_low = sb("wt1_low", [P, 2, H1], F32R)
        wt2_high = sb("wt2_high", [P, H1 // P, H2], F32R)
        wt2_low = sb("wt2_low", [P, H1 // P, H2], F32R)
        wt1 = w2_flat[:, 0:2 * H1].rearrange("p (c n) -> p c n", n=H1)
        wt2 = w2_flat[:, 2 * H1:2 * H1 + H1 // P * H2].rearrange("p (c n) -> p c n", n=H2)
        wt3 = sb("wt3", [P, H2 // P])
        bt1 = sb("bt1", [P, H1 // P])
        bt2 = sb("bt2", [P, H2 // P])
        spare = pairs_high[:, :, :, :].rearrange("p b c n -> p (b c n)")
        p1_high, p1_low, p2_low = spare[:, 0:B], spare[:, B:2 * B], spare[:, 2 * B:3 * B]
        halves = slice(0, BANK), slice(BANK, B)
        half_h1 = H1 // P * BANK
        h1_high = [w2_high[:, a * half_h1:(a + 1) * half_h1].rearrange("p (c n) -> p c n", n=BANK) for a in range(2)]
        h1_low = [w2_low[:, a * half_h1:(a + 1) * half_h1].rearrange("p (c n) -> p c n", n=BANK) for a in range(2)]
        h1_full = pairs[:, :, :].rearrange("p b n -> p (b n)")[:, 0:3 * BANK].rearrange("p (c n) -> p c n", n=BANK)
        h2 = [whole[:, 0:H2 // P * BANK].rearrange("p (c n) -> p c n", n=BANK) for whole in (p1_all, p2_all)]
        top_banks = [turn_bank[:, 1, :], x1_bank[:, :], turn_bank[:, 0, :]]
        p2_banks = [turn_bank[:, 0, :], y_bank[:, 0, :]]
        y_row = w1_flat[0:1, 0:B]

        ids_in = sem("ids_in")
        ident_in = sem("ident_in")
        w1_in = sem("w1_in")
        w2_in = sem("w2_in")
        small_in = sem("small_in")
        wt_in = sem("wt_in")
        gathered = sem("gathered")
        w1_step = sem("w1_step")
        w1_turned = sem("w1_turned")
        w1_rounded = sem("w1_rounded")
        w1_split = sem("w1_split")
        w2_turned = sem("w2_turned")
        w2_rounded = sem("w2_rounded")
        w2_split = sem("w2_split")
        cleared = sem("cleared")
        dense_turned = sem("dense_turned")
        dense_rounded = sem("dense_rounded")
        dense_split = sem("dense_split")
        staged = sem("staged")
        paired = sem("paired")
        turned = sem("turned")
        pairs_rounded = sem("pairs_rounded")
        pairs_split = sem("pairs_split")
        l1_done = sem("l1_done")
        x1_rounded = sem("x1_rounded")
        x1_split = sem("x1_split")
        y_for_act = sem("y_for_act")
        y_for_dve = sem("y_for_dve")
        act_scaled = sem("act_scaled")
        mac_done = sem("mac_done")
        dve_read = sem("dve_read")
        pool_added = sem("pool_added")
        fold_step = sem("fold_step")
        folded = sem("folded")
        p1_reduced = sem("p1_reduced")
        p2_turned = sem("p2_turned")
        wt_rounded = sem("wt_rounded")
        wt_split = sem("wt_split")
        p1_rounded = sem("p1_rounded")
        p1_split = sem("p1_split")
        p2_rounded = sem("p2_rounded")
        p2_split = sem("p2_split")
        h1_split = sem("h1_split")
        top_sum = sem("top_sum")
        top_act = sem("top_act")
        y_out = sem("y_out")

        block = ctx.enter_context(nc.Block())

        @block.sync
        def _(sp):
            sp.dma_start(idx[:, :], ids[0:P, :]).then_inc(ids_in, 16)
            sp.dma_start(w1_ext[:, 0:M, 0:M], W1).then_inc(w1_in, 16)
            sp.dma_start(ident[:, :], eye).then_inc(ident_in, 16)
            sp.dma_start(w2_raw[:, :, :], W2).then_inc(w2_in, 16)
            small = [
                (b1_col[:, :], b1.rearrange("(s o) -> s o", o=1)),
                (b2_row[:, :], b2.rearrange("(o s) -> o s", o=1).to_broadcast([P, S])),
                (wt3[:, :], W_top3.rearrange("(c p) o -> p (c o)", p=P)),
                (bt1[:, :], b_top1.rearrange("(c p) -> p c", p=P)),
                (bt2[:, :], b_top2.rearrange("(c p) -> p c", p=P)),
            ]
            with nc.allow_non_contiguous_dma(reason="a few hundred bias and W_top3 elements"):
                for dst, src in small:
                    sp.dma_start(dst, src).then_inc(small_in, 16)
            sp.wait_ge(cleared, 2)
            for at in range(0, THREE, 32):
                sp.dma_start(dense[:, :, at:at + DC], dense_ctx.rearrange("(t p) c -> p t c", p=P)).then_inc(small_in, 16)
                sp.dma_start(wt1_dense_raw[at:at + DC, :], W_top1[2 * P:2 * P + DC, :]).then_inc(small_in, 16)
            sp.wait_ge(w2_turned, NG)
            sp.dma_start(wt1, W_top1[0:2 * P, :].rearrange("(c p) n -> p c n", p=P)).then_inc(wt_in, 16)
            sp.dma_start(wt2, W_top2.rearrange("(c p) n -> p c n", p=P)).then_inc(wt_in, 16)
            with sp.Fori(0, NB - 1, 1) as i:
                sp.wait_ge(gathered, i * (16 * M) + 16 * M)
                sp.dma_start(idx[:, :], ids[bass.ds(i * P + P, P), :]).then_inc(ids_in, 16)
            sp.wait_ge(top_act, 2 * (H1 // P + H2 // P + 1))
            sp.dma_start(out.rearrange("b o -> o b"), y_row).then_inc(y_out, 16)
            sp.wait_ge(y_out, 16)
        SMALL = 16 * 11

        @block.gpsimd
        def _(pool):
            def gather(f):
                pool.indirect_dma_start(emb[:, f * D:(f + 1) * D], None, tables[f],
                                        bass.IndirectOffsetOnAxis(ap=idx[:, f:f + 1], axis=0)).then_inc(gathered, 16)

            def products(i, t):
                i, t = (i + 1, t - D) if t >= D else (i, t)
                pool.wait_ge(staged, i * 8 + (2 * (t // 4) + 2))
                pool.wait_ge(turned, i * (2 * D) + (2 * t - 2))
                form_products(pool, t).then_inc(paired, 1)

            def add_banks(i, t):
                mine = scaled[:, t % 2]
                dst = pool_sum[:, t % 2, :]
                pool.wait_ge(folded, i * D + (t - 1 + FOLD_CREDIT))
                pool.wait_ge(act_scaled, i * (NA * D) + (NA * t + 2 + ACT_CREDIT))
                pool.tensor_tensor(dst, mine[:, 0, :], mine[:, 1, :], ALU.add).then_inc(pool_added, 1)
                for n in range(2, pool_banks(t)):
                    pool.wait_ge(act_scaled, i * (NA * D) + (NA * t + n + 1 + ACT_CREDIT))
                    pool.wait_ge(pool_added, i * pool_steps(D) + (pool_steps(t) + n - 1))
                    pool.tensor_tensor(dst, dst, mine[:, n, :], ALU.add).then_inc(pool_added, 1)

            def gathers(t):
                n = t - GATHER[0]
                for f in range(M * n // len(GATHER), M * (n + 1) // len(GATHER)):
                    gather(f)

            def body(i, last=False):
                for t in range(D):
                    if not (last and t + PREP >= D):
                        products(i, t + PREP)
                    if not last and t == GATHER[0]:
                        pool.wait_ge(staged, i * 8 + 8)
                        pool.wait_ge(ids_in, i * 16 + 32)
                        pool.tensor_tensor(gate[:, :], b1_col[:, :], b1_col[:, :], ALU.add)
                    if not last and t in GATHER:
                        gathers(t)
                    add_banks(i, t)

            pool.wait_ge(ids_in, 16)
            for f in range(M):
                gather(f)
            pool.wait_ge(small_in, SMALL)
            pool.wait_ge(paired, 2)
            for t in range(2, PREP):
                products(0, t)
            with pool.Fori(0, NB - 1, 1) as i:
                body(i)
            body(NB - 1, last=True)

        @block.tensor
        def _(pe):
            def turn(i, t, half):
                i, t = (i + 1, t - D) if t >= D else (i, t)
                if half == 0:
                    pe.wait_ge(paired, i * D + (t + 1))
                if not (isinstance(i, int) and i == 0 and t <= 2):
                    pe.wait_ge(pairs_split, i * (2 * D) + (2 * t - 1 + half))
                chunks = range(0, 4) if half == 0 else range(4, CH)
                for n, c in enumerate(chunks):
                    mm = pe.transpose(landing(i, t, half)[:, n * P:(n + 1) * P],
                                      pairs[:, t % 2, c * P:(c + 1) * P], ident[:, :])
                mm.then_inc(turned, 1)

            def layer1(i, pair, c):
                i, pair = (i + 1, pair - D // 2) if pair >= D // 2 else (i, pair)
                if c == 0:
                    pe.wait_ge(pairs_split, i * (2 * D) + (4 * pair + 4))
                    if not (isinstance(i, int) and i == 0 and pair == 0):
                        pe.wait_ge(x1_rounded, i * (D // 2) + pair)
                dst = x1_bank[:, 0:2 * P]
                high = pairs_high[:, pair % 2, c, :]
                if c < CH - 1:
                    pe.matmul(dst, w1_low[:, c, :], high, start=(c == 0), stop=False)
                    pe.matmul(dst, w1_high[:, c, :], pairs_low[:, pair % 2, c, :], start=False, stop=False)
                    pe.matmul(dst, w1_high[:, c, :], high, start=False, stop=False)
                else:
                    pe.matmul(dst, w1_high[:, c, :], high, start=False, stop=True).then_inc(l1_done, 1)

            def layer2(i, t, q):
                bank, n = q % RING, S * len(fields(q))
                if q == 0 and t % 2 == 0:
                    pe.wait_ge(x1_split, i * (D // 2) + (t // 2 + 1))
                before, n_t = (q - RING, t) if q >= RING else (q + RING, t - 1)
                if before in act_banks:
                    pe.wait_ge(act_scaled, i * (NA * D) + (NA * n_t + act_banks.index(before) + 1 + ACT_CREDIT))
                else:
                    pe.wait_ge(dve_read, i * (NV * D) + (NV * n_t + dve_banks.index(before) + 1 + DVE_CREDIT))
                cols = slice(MB * S * q, MB * S * q + n)
                high = x1_high[:, t // 2 % 2, t % 2 * P:(t % 2 + 1) * P]
                low = x1_low[:, t // 2 % 2, t % 2 * P:(t % 2 + 1) * P]
                dst = y_bank[:, bank, 0:n]
                pe.matmul(dst, low, w2_high[:, cols], start=True, stop=False)
                pe.matmul(dst, high, w2_low[:, cols], start=False, stop=False)
                mm = pe.matmul(dst, high, w2_high[:, cols], start=False, stop=True)
                mm.then_inc(y_for_act if q in act_banks else y_for_dve, 1)

            BEHIND = [
                {2: ("turn", 0), 4: ("l1", 0), 5: ("turn", 1), 6: ("l1", 1), 7: ("l1", 2), 9: ("l1", 3)},
                {0: ("l1", 4), 2: ("turn", 0), 1: ("l1", 5), 3: ("l1", 6), 5: ("turn", 1)},
            ]

            def turn_p2(half):
                pe.wait_ge(folded, (half + 1) * (NB // 2 * D) + FOLD_CREDIT)
                for n in range(NB // 2):
                    b = half * NB // 2 + n
                    mm = pe.transpose(p2_banks[half][:, n * P:(n + 1) * P], p2_all[:, b * S:(b + 1) * S], ident[:, :])
                mm.then_inc(p2_turned, 1)

            def body(i, last=False):
                for t in range(D):
                    for q in range(NG):
                        layer2(i, t, q)
                        what, n = BEHIND[t % 2].get(q, (None, 0))
                        if what == "l1" and not (last and t // 2 + 1 >= D // 2):
                            layer1(i, t // 2 + 1, n)
                        if what == "turn" and not (last and t + PREP >= D):
                            turn(i, t + PREP, n)
                        if last and t == D - 4 and q == 7:
                            turn_p2(0)

            pe.wait_ge(ident_in, 16)
            pe.wait_ge(w2_in, 16)
            for q in range(NG):
                if q >= RING:
                    pe.wait_ge(w2_split, q - RING + 1)
                for n, m in enumerate(fields(q)):
                    mm = pe.transpose(y_bank[:, q % RING, n * P:(n + 1) * P], w2_raw[:, :, m], ident[:, :])
                mm.then_inc(w2_turned, 1)
            pe.wait_ge(w1_step, 7)
            for c in range(CH):
                mm = pe.transpose(turn_bank[:, c // 4, c % 4 * P:(c % 4 + 1) * P],
                                  w1_fold[:, c * P:(c + 1) * P], ident[:, :])
            mm.then_inc(w1_turned, 1)
            pe.wait_ge(small_in, SMALL)
            for half in range(2):
                if half:
                    pe.wait_ge(dense_split, 1)
                for n in range(NB // 2):
                    mm = pe.transpose(x1_bank[0:THREE, n * P:(n + 1) * P], dense[:, half * NB // 2 + n, :], ident[:, :])
                mm.then_inc(dense_turned, 1)
            pe.wait_ge(w1_split, 2)
            pe.wait_ge(w2_split, NG)
            pe.wait_ge(dense_split, 2)
            for t in range(3):
                turn(0, t, 0)
                turn(0, t, 1)
            for c in range(CH):
                layer1(0, 0, c)
            turn(0, 3, 0)
            turn(0, 3, 1)
            with pe.Fori(0, NB - 1, 1) as i:
                body(i)
            body(NB - 1, last=True)

            step = 0

            def next_bank():
                if step >= len(top_banks):
                    pe.wait_ge(top_act, step - len(top_banks) + 1)
                return top_banks[step % len(top_banks)]

            def three(dst, w_high, w_low, high, low, start, stop):
                pe.matmul(dst, w_low, high, start=start, stop=False)
                pe.matmul(dst, w_high, low, start=False, stop=False)
                return pe.matmul(dst, w_high, high, start=False, stop=stop)

            pe.wait_ge(wt_split, 3)
            for half in range(2):
                pe.wait_ge(p1_split, half + 1)
                rows = slice(half * BANK, (half + 1) * BANK)
                for c in range(H1 // P):
                    if half == 0 and c == H1 // P - 1:
                        pe.wait_ge(act_scaled, NB * NA * D + ACT_CREDIT)
                        turn_p2(1)
                    dst = next_bank()
                    cols = slice(c * P, (c + 1) * P)
                    three(dst, wt1_high[:, 0, cols], wt1_low[:, 0, cols], p1_high[:, rows], p1_low[:, rows], True, False)
                    pe.matmul(dst, wt1_dense[:, cols], dense_t[:, rows], start=False, stop=False)
                    if c == 0:
                        pe.wait_ge(p2_split, half + 1)
                    three(dst, wt1_high[:, 1, cols], wt1_low[:, 1, cols], p2_high[:, rows], p2_low[:, rows], False,
                          True).then_inc(top_sum, 1)
                    step += 1
            for half in range(2):
                for c in range(H2 // P):
                    dst = next_bank()
                    cols = slice(c * P, (c + 1) * P)
                    for k in range(H1 // P):
                        if c == 0:
                            pe.wait_ge(h1_split, half * (H1 // P) + k + 1)
                        mm = three(dst, wt2_high[:, k, cols], wt2_low[:, k, cols], h1_high[half][:, k, :],
                                   h1_low[half][:, k, :], k == 0, k == H1 // P - 1)
                    mm.then_inc(top_sum, 1)
                    step += 1
            for half in range(2):
                pe.wait_ge(top_act, 2 * (H1 // P) + (half + 1) * (H2 // P))
                dst = next_bank()
                for k in range(H2 // P):
                    mm = pe.matmul(dst[0:1, :], wt3[:, k:k + 1], h2[half][:, k, :],
                                   start=(k == 0), stop=(k == H2 // P - 1))
                mm.then_inc(top_sum, 1)
                step += 1

        @block.scalar
        def _(act):
            def scale(i, t, a):
                q = act_banks[a]
                if a == 0:
                    act.wait_ge(folded, i * D + (t - 1 + FOLD_CREDIT))
                act.wait_ge(y_for_act, i * (NA * D) + (NA * t + a + 1))
                for n, m in enumerate(fields(q)):
                    ins = act.activation(scaled[:, t % 2, a, n * S:(n + 1) * S], y_bank[:, q % RING, n * S:(n + 1) * S],
                                         ACT.Copy, scale=x0[:, t // 4, t % 4, m:m + 1])
                ins.then_inc(act_scaled, 1)

            def pairs_to_high(i, t, half):
                i, t = (i + 1, t - D) if t >= D else (i, t)
                act.wait_ge(turned, i * (2 * D) + (2 * t + half + 1))
                if t % 2 == 0 and half == 0 and not (isinstance(i, int) and i == 0 and t < 4):
                    act.wait_ge(l1_done, i * (D // 2) + (t // 2 - 1))
                c0, c1 = (0, 4) if half == 0 else (4, CH)
                act.activation(pairs_high[:, t // 2 % 2, c0:c1, t % 2 * P:(t % 2 + 1) * P],
                               landing(i, t, half)[:, 0:(c1 - c0) * P].rearrange("p (c n) -> p c n", n=P),
                               ACT.Copy).then_inc(pairs_rounded, 1)

            def first_maps(i, pair):
                i, pair = (i + 1, pair - D // 2) if pair >= D // 2 else (i, pair)
                act.wait_ge(l1_done, i * (D // 2) + (pair + 1))
                if pair == 0 and not (isinstance(i, int) and i == 0):
                    act.wait_ge(p1_reduced, i * 4)
                act.activation(x1_full[:, 2 * pair:2 * pair + 2, :],
                               x1_bank[:, 0:2 * P].rearrange("p (d n) -> p d n", n=P),
                               ACT.Relu, bias=b1_col[:, 0:1])
                act.activation(x1_high[:, pair % 2, :], x1_bank[:, 0:2 * P],
                               ACT.Relu, bias=b1_col[:, 0:1]).then_inc(x1_rounded, 1)

            def p1_to_high(part):
                act.wait_ge(p1_reduced, 4 * (NB // 2) * (part + 1))
                act.activation(p1_high[:, halves[part]], p1_all[:, halves[part]], ACT.Copy).then_inc(p1_rounded, 1)

            def p2_to_high(half):
                act.wait_ge(p2_turned, half + 1)
                act.activation(p2_high[:, half * BANK:(half + 1) * BANK], p2_banks[half],
                               ACT.Copy).then_inc(p2_rounded, 1)

            BEHIND = [
                {1: ("high", 0), 5: ("high", 1)},
                {1: ("high", 0), 3: ("maps", 0), 5: ("high", 1)},
            ]

            def body(i, last=False):
                for t in range(D):
                    for a in range(NA):
                        scale(i, t, a)
                        what, n = BEHIND[t % 2].get(a, (None, 0))
                        if what == "maps" and not (last and t // 2 + 1 >= D // 2):
                            first_maps(i, t // 2 + 1)
                        if what == "high" and not (last and t + PREP >= D):
                            pairs_to_high(i, t + PREP, n)
                    if last and t == D - 4:
                        p2_to_high(0)
                    if last and t == D - 3:
                        p1_to_high(0)

            act.sem_inc(act_scaled, ACT_CREDIT)
            for q in range(NG):
                act.wait_ge(w2_turned, q + 1)
                n = S * len(fields(q))
                act.activation(w2_high[:, MB * S * q:MB * S * q + n], y_bank[:, q % RING, 0:n],
                               ACT.Copy).then_inc(w2_rounded, 1)
            act.wait_ge(w1_turned, 1)
            for half, (c0, c1) in enumerate([(0, 4), (4, CH)]):
                src = turn_bank[:, half, 0:(c1 - c0) * P].rearrange("p (c n) -> p c n", n=P)
                act.activation(w1_high[:, c0:c1, :], src, ACT.Copy).then_inc(w1_rounded, 1)
            act.wait_ge(small_in, SMALL)
            for half in range(2):
                act.wait_ge(dense_turned, half + 1)
                act.activation(dense_t[:, half * BANK:(half + 1) * BANK], x1_bank[0:THREE, :],
                               ACT.Copy).then_inc(dense_rounded, 1)
            act.activation(wt1_dense[:, :], wt1_dense_raw, ACT.Copy).then_inc(wt_rounded, 1)
            act.wait_ge(wt_in, 32)
            act.activation(wt1_high[:, :, :], wt1, ACT.Copy).then_inc(wt_rounded, 1)
            act.activation(wt2_high[:, :, :], wt2, ACT.Copy).then_inc(wt_rounded, 1)
            for t in range(PREP):
                if t == PREP - 1:
                    first_maps(0, 0)
                pairs_to_high(0, t, 0)
                pairs_to_high(0, t, 1)
            with act.Fori(0, NB - 1, 1) as i:
                body(i)
            body(NB - 1, last=True)

            step = 0

            def take(dst, func, **bias):
                act.wait_ge(top_sum, step + 1)
                src = top_banks[step % len(top_banks)]
                act.activation(dst, src[0:dst.shape[0], :], func, **bias).then_inc(top_act, 1)

            p1_to_high(1)
            for half in range(2):
                for c in range(H1 // P):
                    if half == 0 and c == H1 // P - 1:
                        p2_to_high(1)
                    act.wait_ge(top_sum, step + 1)
                    if step >= 3:
                        act.wait_ge(h1_split, step - 2)
                    src, bias = top_banks[step % len(top_banks)], bt1[:, c:c + 1]
                    act.activation(h1_full[:, step % 3, :], src, ACT.Relu, bias=bias)
                    act.activation(h1_high[half][:, c, :], src, ACT.Relu, bias=bias).then_inc(top_act, 1)
                    step += 1
            for half in range(2):
                for c in range(H2 // P):
                    take(h2[half][:, c, :], ACT.Relu, bias=bt2[:, c:c + 1])
                    step += 1
            for half in range(2):
                take(y_row[:, half * BANK:(half + 1) * BANK], ACT.Copy)
                step += 1

        @block.vector
        def _(dve):
            def macs(i, t, v, part):
                i, t = (i + 1, t - D) if t >= D else (i, t)
                q = dve_banks[v]
                if part == 0:
                    dve.wait_ge(y_for_dve, i * (NV * D) + (NV * t + v + 1))
                for n in (2 * part, 2 * part + 1):
                    m = MB * q + n
                    src = y_bank[:, q % RING, n * S:(n + 1) * S]
                    dst = mac[:, t % 2, n % 2 * S:(n % 2 + 1) * S]
                    x = x0[:, t // 4, t % 4, m:m + 1]
                    if v == 0 and n == 1:
                        ins = dve.tensor_scalar(dst, src, x, None, ALU.mult)
                    else:
                        if n == 1:
                            dve.wait_ge(dve_read, i * (NV * D) + (NV * t + v + DVE_CREDIT))
                        elif v or n:
                            dve.wait_ge(mac_done, i * (3 * NV * D) + (3 * NV * t + 3 * v + max(n - 1, 0)))
                        first = b2_row[:, :] if v == 0 and n == 0 else dst
                        ins = dve.scalar_tensor_tensor(out=dst, in0=src, scalar=x, in1=first,
                                                       op0=ALU.mult, op1=ALU.add)
                    if n < 3:
                        ins.then_inc(mac_done, 1)
                    else:
                        ins.then_inc(dve_read, 1)

            def fold(i, t, step):
                mine = scaled[:, t % 2]
                first = pool_banks(t)
                banks = NA - first
                if step > banks + 3:
                    return
                if step:
                    dve.wait_ge(fold_step, i * fold_steps(D) + (fold_steps(t) + step))
                if step == 0:
                    dve.wait_ge(act_scaled, i * (NA * D) + (NA * t + first + 2 + ACT_CREDIT))
                    dve.tensor_tensor(fold4[:, :], mine[:, first, :], mine[:, first + 1, :],
                                      ALU.add).then_inc(fold_step, 1)
                elif step < banks - 1:
                    a = first + 1 + step
                    n = S * len(fields(act_banks[a]))
                    dve.wait_ge(act_scaled, i * (NA * D) + (NA * t + a + 1 + ACT_CREDIT))
                    dve.tensor_tensor(fold4[:, 0:n], fold4[:, 0:n], mine[:, a, 0:n], ALU.add).then_inc(fold_step, 1)
                elif step == banks - 1:
                    dve.wait_ge(pool_added, i * pool_steps(D) + pool_steps(t + 1))
                    dve.tensor_tensor(fold4[:, :], fold4[:, :], pool_sum[:, t % 2, :], ALU.add).then_inc(fold_step, 1)
                elif step == banks:
                    dve.tensor_tensor(fold2[:, :], fold4[:, 0:2 * S], fold4[:, 2 * S:4 * S],
                                      ALU.add).then_inc(fold_step, 1)
                elif step == banks + 1:
                    dve.wait_ge(dve_read, i * (NV * D) + (NV * t + NV + DVE_CREDIT))
                    dve.tensor_tensor(fold2[:, :], fold2[:, :], mac[:, t % 2, :], ALU.add).then_inc(fold_step, 1)
                elif step == banks + 2:
                    dve.tensor_tensor(fold1[:, :], fold2[:, 0:S], fold2[:, S:2 * S], ALU.add).then_inc(fold_step, 1)
                elif t == 0:
                    dve.tensor_scalar(p2_part[:, :], fold1[:, :], 0.0, None, ALU.max).then_inc(folded, 1)
                else:
                    dve.wait_ge(folded, i * D + (t + FOLD_CREDIT))
                    dst = p2_part[:, :] if t < D - 1 else p2_all[:, bass.ds(i * S, S)]
                    dve.scalar_tensor_tensor(out=dst, in0=fold1[:, :], scalar=0.0, in1=p2_part[:, :],
                                             op0=ALU.max, op1=ALU.add).then_inc(folded, 1)

            def pairs_to_low(i, t, half):
                i, t = (i + 1, t - D) if t >= D else (i, t)
                dve.wait_ge(pairs_rounded, i * (2 * D) + (2 * t + half + 1))
                cols = slice(t % 2 * P, (t % 2 + 1) * P)
                c0, c1 = (0, 4) if half == 0 else (4, CH - 1)
                src = landing(i, t, half)
                ins = dve.tensor_tensor(pairs_low[:, t // 2 % 2, c0:c1, cols],
                                        src[:, 0:(c1 - c0) * P].rearrange("p (c n) -> p c n", n=P),
                                        pairs_high[:, t // 2 % 2, c0:c1, cols].bitcast(F32), ALU.subtract)
                if half:
                    low = pairs_high[32:64, t // 2 % 2, CH - 1, cols]
                    ins = dve.tensor_tensor(low, src[32:64, (c1 - c0) * P:(CH - c0) * P], low.bitcast(F32),
                                            ALU.subtract)
                ins.then_inc(pairs_split, 1)

            def sum_p1(i, part):
                n = P // 4
                ins = dve.tensor_reduce(p1_all[:, bass.ds(i * P + part * n, n)],
                                        x1_full[:, :, part * n:(part + 1) * n].rearrange("p d n -> p n d"),
                                        AX_X, ALU.add)
                ins.then_inc(p1_reduced, 1)

            def stage(g):
                src = emb[:, :].rearrange("p (m d) -> p d m", d=D)[:, 4 * g:4 * g + 4, :]
                dve.tensor_copy(x0[:, g, :, 0:M], src).then_inc(staged, 1)
                dve.tensor_copy(x0[:, g, :, M:EXT], src[:, :, 0:EXT - M]).then_inc(staged, 1)

            def low_part(i, pair):
                i, pair = (i + 1, pair - D // 2) if pair >= D // 2 else (i, pair)
                dve.wait_ge(x1_rounded, i * (D // 2) + (pair + 1))
                full = x1_full[:, 2 * pair:2 * pair + 2, :].rearrange("p d n -> p (d n)")
                dve.tensor_tensor(x1_low[:, pair % 2, :], full, x1_high[:, pair % 2, :].bitcast(F32),
                                  ALU.subtract).then_inc(x1_split, 1)

            ORDER = [
                [("fold", 0), ("low", 1), ("fold", 1), ("mac", 0, 0), ("fold", 2), ("mac", 0, 1), ("fold", 3),
                 ("low", 0), ("mac", 1, 0), ("fold", 4), ("mac", 1, 1), ("stage",), ("x1",), ("p1", 0),
                 ("fold", 5), ("mac", 2, 0), ("fold", 6), ("mac", 2, 1), ("fold", 7), ("fold", 8), ("p1", 1)],
                [("fold", 0), ("low", 1), ("fold", 1), ("mac", 0, 0), ("fold", 2), ("mac", 0, 1), ("fold", 3),
                 ("low", 0), ("mac", 1, 0), ("fold", 4), ("mac", 1, 1), ("stage",), ("p1", 0),
                 ("fold", 5), ("mac", 2, 0), ("fold", 6), ("mac", 2, 1), ("fold", 7), ("fold", 8), ("p1", 1)],
            ]
            STAGE = {10: 0, 11: 1, 12: 2}
            P1 = {(D - 4, 0): 0, (D - 4, 1): 1, (D - 3, 0): 2, (D - 3, 1): 3}

            def p1_to_low(part):
                dve.wait_ge(p1_rounded, part + 1)
                rows = halves[part]
                dve.tensor_tensor(p1_low[:, rows], p1_all[:, rows], p1_high[:, rows].bitcast(F32),
                                  ALU.subtract).then_inc(p1_split, 1)

            def p2_to_low(half):
                dve.wait_ge(p2_rounded, half + 1)
                rows = slice(half * BANK, (half + 1) * BANK)
                dve.tensor_tensor(p2_low[:, rows], p2_banks[half], p2_high[:, rows].bitcast(F32),
                                  ALU.subtract).then_inc(p2_split, 1)

            def body(i, last=False):
                stage(3)
                for t in range(D):
                    for what, *n in ORDER[t % 2]:
                        if what == "mac" and not (last and t == D - 1):
                            macs(i, t + 1, *n)
                        if what == "fold":
                            fold(i, t, *n)
                        if what == "low":
                            ahead = t + PREP + (1 - n[0])
                            if not (last and ahead >= D):
                                pairs_to_low(i, ahead, *n)
                        if what == "x1" and not (last and t == D - 2):
                            low_part(i, t // 2 + 1)
                        if what == "p1" and (t, *n) in P1:
                            sum_p1(i, P1[(t, *n)])
                        if what == "stage" and not last and t in STAGE:
                            if STAGE[t] == 0:
                                dve.wait_ge(gathered, i * (16 * M) + 32 * M)
                            stage(STAGE[t])
                    if last and t == D - 4:
                        p2_to_low(0)
                    if last and t == D - 3:
                        p1_to_low(0)

            dve.sem_inc(dve_read, DVE_CREDIT)
            dve.sem_inc(folded, FOLD_CREDIT)
            dve.memset(scaled[:, 0, 0:2, :], 0.0).then_inc(cleared, 1)
            dve.memset(wt1_dense_raw, 0.0).then_inc(cleared, 1)
            dve.memset(pairs[:, :, PAIRS:CH * P], 0.0).then_inc(w1_step, 1)
            dve.memset(w1_fold[:, PAIRS:CH * P], 0.0).then_inc(w1_step, 1)
            dve.wait_ge(w1_in, 16)
            W = EXT - M
            dve.tensor_copy(w1_ext[:, 0:M, M:EXT], w1_ext[:, 0:M, 0:W]).then_inc(w1_step, 1)
            dve.tensor_copy(w1_ext[:, M:EXT, 0:M], w1_ext[:, 0:W, 0:M]).then_inc(w1_step, 1)
            flat = w1_ext[:, 0, 0:M]
            part = list(flat.ap[0])
            over = bass.AP(flat.tensor, flat.offset + 1, [part, [1, SHIFTS - 1], [EXT + 1, M]])
            under = bass.AP(flat.tensor, flat.offset + EXT, [part, [EXT, SHIFTS - 1], [EXT + 1, M]])
            diag = bass.AP(flat.tensor, flat.offset, [part, [EXT + 1, M]])
            dve.tensor_copy(w1_fold[:, 0:M], diag).then_inc(w1_step, 1)
            dve.wait_ge(w1_step, 4)
            dve.tensor_tensor(w1_fold[:, M:PAIRS].rearrange("p (k h) -> p k h", h=M), over, under,
                              ALU.add).then_inc(w1_step, 1)
            dve.wait_ge(w1_step, 6)
            rest = w1_fold[:, LAST:PAIRS].unsqueeze(1).to_broadcast([P, 2, REST])
            dve.tensor_copy(copies(w1_fold), rest).then_inc(w1_step, 1)
            dve.wait_ge(small_in, SMALL)
            for q in range(NG):
                dve.wait_ge(w2_rounded, q + 1)
                n = S * len(fields(q))
                cols = slice(MB * S * q, MB * S * q + n)
                dve.tensor_tensor(w2_low[:, cols], y_bank[:, q % RING, 0:n], w2_high[:, cols].bitcast(F32),
                                  ALU.subtract).then_inc(w2_split, 1)
            for half, (c0, c1) in enumerate([(0, 4), (4, CH)]):
                dve.wait_ge(w1_rounded, half + 1)
                c1 = min(c1, CH - 1)
                src = turn_bank[:, half, 0:(c1 - c0) * P].rearrange("p (c n) -> p c n", n=P)
                ins = dve.tensor_tensor(w1_low[:, c0:c1, :], src, w1_high[:, c0:c1, :].bitcast(F32), ALU.subtract)
                if half:
                    low = w1_high[0:32, CH - 1, :]
                    ins = dve.tensor_tensor(low, turn_bank[0:32, half, (c1 - c0) * P:(CH - c0) * P],
                                            low.bitcast(F32), ALU.subtract)
                ins.then_inc(w1_split, 1)
            for half in range(2):
                dve.wait_ge(dense_rounded, half + 1)
                low = dense_t[32:64, half * BANK:(half + 1) * BANK]
                dve.tensor_tensor(low, x1_bank[32:64, :], low.bitcast(F32), ALU.subtract).then_inc(dense_split, 1)
            dve.wait_ge(wt_rounded, 1)
            low = wt1_dense[0:32, :]
            dve.tensor_tensor(low, wt1_dense_raw[0:32, :], low.bitcast(F32), ALU.subtract).then_inc(wt_split, 1)
            dve.wait_ge(wt_rounded, 2)
            dve.tensor_tensor(wt1_low[:, :, :], wt1, wt1_high[:, :, :].bitcast(F32), ALU.subtract).then_inc(wt_split, 1)
            dve.wait_ge(wt_rounded, 3)
            dve.tensor_tensor(wt2_low[:, :, :], wt2, wt2_high[:, :, :].bitcast(F32), ALU.subtract).then_inc(wt_split, 1)
            dve.wait_ge(gathered, 16 * M)
            stage(0)
            for t in range(2):
                dve.wait_ge(staged, 2)
                form_products(dve, t).then_inc(paired, 1)
            stage(1)
            stage(2)
            for t in range(PREP):
                if t == PREP - 1:
                    low_part(0, 0)
                pairs_to_low(0, t, 0)
                pairs_to_low(0, t, 1)
            for v in range(NV):
                macs(0, 0, v, 0)
                macs(0, 0, v, 1)
                if v == 1:
                    pairs_to_low(0, PREP, 0)
            with dve.Fori(0, NB - 1, 1) as i:
                body(i)
            body(NB - 1, last=True)
            p1_to_low(1)
            for half in range(2):
                for c in range(H1 // P):
                    if half == 0 and c == H1 // P - 1:
                        p2_to_low(1)
                    step = half * (H1 // P) + c
                    dve.wait_ge(top_act, step + 1)
                    dve.tensor_tensor(h1_low[half][:, c, :], h1_full[:, step % 3, :], h1_high[half][:, c, :].bitcast(F32),
                                      ALU.subtract).then_inc(h1_split, 1)


_TABLES = [f"tbl_{n}" for n in range(39)]
_INS = (["dense_ctx", "ids"] + _TABLES + ["W_top1", "b_top1", "W_top2", "b_top2", "W_top3",
        "L0_rec_W1", "L0_rec_b1", "L0_rec_W2", "L0_rec_b2"])


def kernel(**inputs):
    import numpy as _np
    import concourse.bacc as _bacc
    from concourse import mybir as _mybir
    from concourse.bass_utils import run_bass_kernel_spmd as _run

    nc = _bacc.Bacc("TRN2", target_bir_lowering=False, num_devices=1)
    arrays, aps = {}, {}
    for name in _INS + ["identity"]:
        a = _np.eye(128, dtype=_np.float32) if name == "identity" else _np.ascontiguousarray(inputs[name])
        arrays[f"in_{name}"] = a
        aps[name] = nc.dram_tensor(f"in_{name}", a.shape, _mybir.dt.from_np(a.dtype), kind="ExternalInput").ap()
    rows = inputs["ids"].shape[0]
    out = nc.dram_tensor("out_y", (rows, 1), _mybir.dt.float32, kind="ExternalOutput").ap()
    ids = aps["ids"].bitcast(_mybir.dt.uint32)
    build(nc, aps["dense_ctx"], ids, [aps[n] for n in _TABLES], aps["W_top1"], aps["b_top1"], aps["W_top2"],
          aps["b_top2"], aps["W_top3"], aps["L0_rec_W1"], aps["L0_rec_b1"], aps["L0_rec_W2"], aps["L0_rec_b2"],
          aps["identity"], out)
    r = _run(nc, [arrays], core_ids=[0])
    return r.results[0]["out_y"]
```
